# Optimizing a Trainium2 kernel written in Bass

```python
import numpy as np
import jax
import jax.numpy as jnp

def _softmax(x, axis=-1):
    return jax.nn.softmax(x, axis=axis)

def _gelu(x):
    return jax.nn.gelu(x, approximate=True)

def _silu(x):
    return jax.nn.silu(x)

def _sigmoid(x):
    return jax.nn.sigmoid(x)

def _layernorm(x, axis=-1, eps=1e-05):
    m = jnp.mean(x, axis=axis, keepdims=True)
    v = jnp.var(x, axis=axis, keepdims=True)
    return (x - m) / jnp.sqrt(v + eps)

def _scatter_add(tgt, idx, src, axis=0):
    return tgt.at[idx].add(src)

def _segment_sum(src, seg, n):
    return jax.ops.segment_sum(src, seg, n)
kernel_name = 'mk_xattn_ffn_d1_seqx_r8_edcace'

def setup_inputs(seed: int=0):
    np.random.seed(seed)
    _w = jnp.asarray

    def _rec_inputs():
        import jax
        import jax.numpy as jnp
        _rk = jax.random.key(seed)
        x = 7.22e-05 + 1 * jax.random.normal(jax.random.fold_in(_rk, 1), (2, 512, 128), jnp.float32)
        _lenS = 512 - jax.random.randint(jax.random.fold_in(_rk, 7), (2,), 0, max(1, 512 // 4) + 1, jnp.int32)
        _lenS2 = 32 - jax.random.randint(jax.random.fold_in(_rk, 8), (2,), 0, max(1, 32 // 4) + 1, jnp.int32)
        _ctx_768P = jax.random.normal(jax.random.fold_in(_rk, 11), (2, 16, 96), jnp.float32)
        _ctx_768c = jax.random.dirichlet(jax.random.fold_in(_rk, 511), 0.3 * jnp.ones((16,), jnp.float32), (2, 32))
        _ctx_768t = jnp.einsum('bsk,bkd->bsd', _ctx_768c, _ctx_768P)
        _ctx_768t = _ctx_768t * jax.lax.rsqrt(jnp.mean(jnp.square(_ctx_768t)) + 1e-12) * 0.953939
        ctx_768 = 2.09791e-05 + 1.00001 * (_ctx_768t + 0.3 * jax.random.normal(jax.random.fold_in(_rk, 611), (2, 32, 96), jnp.float32))
        return (x, ctx_768)
    x, ctx_768 = _rec_inputs()

    def _L0_xattn_setup():
        import jax, jax.numpy as jnp
        import numpy as np
        IN_DIM = 128
        CTX_DIM = 96
        NUM_HEADS = 16
        HEAD_DIM = IN_DIM // NUM_HEADS
        SCALE = 1.0 / float(np.sqrt(HEAD_DIM))
        key = jax.random.key(seed)
        ks = jax.random.split(key, 10)
        B, NQ, NKV = (8, 128, 64)
        s_in = 1.0 / float(np.sqrt(IN_DIM))
        s_ctx = 1.0 / float(np.sqrt(CTX_DIM))
        return {'x': jax.random.normal(ks[0], (B, NQ, IN_DIM), dtype=jnp.float32), 'context': jax.random.normal(ks[1], (B, NKV, CTX_DIM), dtype=jnp.float32), 'Wq': jax.random.normal(ks[2], (IN_DIM, IN_DIM), dtype=jnp.float32) * s_in, 'bq': jax.random.normal(ks[3], (IN_DIM,), dtype=jnp.float32) * 0.01, 'Wk': jax.random.normal(ks[4], (IN_DIM, CTX_DIM), dtype=jnp.float32) * s_ctx, 'bk': jax.random.normal(ks[5], (IN_DIM,), dtype=jnp.float32) * 0.01, 'Wv': jax.random.normal(ks[6], (IN_DIM, CTX_DIM), dtype=jnp.float32) * s_ctx, 'bv': jax.random.normal(ks[7], (IN_DIM,), dtype=jnp.float32) * 0.01, 'Wo': jax.random.normal(ks[8], (IN_DIM, IN_DIM), dtype=jnp.float32) * s_in, 'bo': jax.random.normal(ks[9], (IN_DIM,), dtype=jnp.float32) * 0.01}
    _L0_xattn_all = _L0_xattn_setup()
    _L0_xattn_in = {k: v for k, v in _L0_xattn_all.items() if k in ('Wq', 'bq', 'Wk', 'bk', 'Wv', 'bv', 'Wo', 'bo')}
    del _L0_xattn_all

    def _L0_ffn_setup():
        import jax, jax.numpy as jnp
        import numpy as np
        H = 128
        I = 128
        E = 16
        K = 4
        LIMIT = 7.0
        ALPHA = 1.702
        EPS = 1e-05
        key = jax.random.key(seed)
        ks = jax.random.split(key, 8)
        x = jax.random.normal(ks[0], (2, 64, H), dtype=jnp.float32)
        norm_scale = jnp.ones((H,), dtype=jnp.float32)
        wg = jax.random.normal(ks[1], (H, E), dtype=jnp.float32) * 0.02
        bg = jax.random.normal(ks[2], (E,), dtype=jnp.float32) * 0.02
        w1 = jax.random.normal(ks[3], (E, H, 2 * I), dtype=jnp.float32) * 0.02
        b1 = jax.random.normal(ks[4], (E, 2 * I), dtype=jnp.float32) * 0.02
        w2 = jax.random.normal(ks[5], (E, I, H), dtype=jnp.float32) * 0.02
        b2 = jax.random.normal(ks[6], (E, H), dtype=jnp.float32) * 0.02
        return {'x': x, 'norm_scale': norm_scale, 'wg': wg, 'bg': bg, 'w1': w1, 'b1': b1, 'w2': w2, 'b2': b2}
    _L0_ffn_all = _L0_ffn_setup()
    _L0_ffn_in = {k: v for k, v in _L0_ffn_all.items() if k in ('norm_scale', 'wg', 'bg', 'w1', 'b1', 'w2', 'b2')}
    del _L0_ffn_all
    return {'x': x, 'ctx_768': ctx_768, 'L0_xattn_Wq': _L0_xattn_in['Wq'], 'L0_xattn_bq': _L0_xattn_in['bq'], 'L0_xattn_Wk': _L0_xattn_in['Wk'], 'L0_xattn_bk': _L0_xattn_in['bk'], 'L0_xattn_Wv': _L0_xattn_in['Wv'], 'L0_xattn_bv': _L0_xattn_in['bv'], 'L0_xattn_Wo': _L0_xattn_in['Wo'], 'L0_xattn_bo': _L0_xattn_in['bo'], 'L0_ffn_norm_scale': _L0_ffn_in['norm_scale'], 'L0_ffn_wg': _L0_ffn_in['wg'], 'L0_ffn_bg': _L0_ffn_in['bg'], 'L0_ffn_w1': _L0_ffn_in['w1'], 'L0_ffn_b1': _L0_ffn_in['b1'], 'L0_ffn_w2': _L0_ffn_in['w2'], 'L0_ffn_b2': _L0_ffn_in['b2']}

def reference(x, ctx_768, L0_xattn_Wq, L0_xattn_bq, L0_xattn_Wk, L0_xattn_bk, L0_xattn_Wv, L0_xattn_bv, L0_xattn_Wo, L0_xattn_bo, L0_ffn_norm_scale, L0_ffn_wg, L0_ffn_bg, L0_ffn_w1, L0_ffn_b1, L0_ffn_w2, L0_ffn_b2):
    import jax
    import jax.numpy as jnp

    def _L0_xattn_ref(x, context, Wq, bq, Wk, bk, Wv, bv, Wo, bo):
        import jax, jax.numpy as jnp
        import numpy as np
        IN_DIM = 128
        CTX_DIM = 96
        NUM_HEADS = 16
        HEAD_DIM = IN_DIM // NUM_HEADS
        SCALE = 1.0 / float(np.sqrt(HEAD_DIM))
        q = x @ Wq.T + bq
        k = context @ Wk.T + bk
        v = context @ Wv.T + bv
        B, NQ, _ = q.shape
        NKV = k.shape[1]
        q = q.reshape(B, NQ, NUM_HEADS, HEAD_DIM)
        k = k.reshape(B, NKV, NUM_HEADS, HEAD_DIM)
        v = v.reshape(B, NKV, NUM_HEADS, HEAD_DIM)
        attn = jnp.einsum('bihd,bjhd->bhij', q, k) * SCALE
        attn = jax.nn.softmax(attn, axis=-1)
        out = jnp.einsum('bhij,bjhd->bihd', attn, v)
        out = out.reshape(B, NQ, IN_DIM)
        return out @ Wo.T + bo

    def _L0_ffn_ref(x, norm_scale, wg, bg, w1, b1, w2, b2):
        import jax, jax.numpy as jnp
        import numpy as np
        H = 128
        I = 128
        E = 16
        K = 4
        LIMIT = 7.0
        ALPHA = 1.702
        EPS = 1e-05
        shape = x.shape
        xf = x.reshape(-1, shape[-1])
        xn = xf * jax.lax.rsqrt(jnp.mean(xf * xf, axis=-1, keepdims=True) + EPS) * norm_scale
        logits = xn @ wg + bg
        vals, idx = jax.lax.top_k(logits, K)
        gates = jax.nn.softmax(vals, axis=-1)
        gate_full = jnp.einsum('tke,tk->te', jax.nn.one_hot(idx, E, dtype=gates.dtype), gates)
        h = jnp.einsum('th,ehd->etd', xn, w1) + b1[:, None, :]
        a = jnp.minimum(h[..., ::2], LIMIT)
        b = jnp.clip(h[..., 1::2], -LIMIT, LIMIT)
        s = a * jax.nn.sigmoid(ALPHA * a) * (b + 1.0)
        y = jnp.einsum('eti,eih->eth', s, w2) + b2[:, None, :]
        t = jnp.einsum('eth,te->th', y, gate_full)
        return x + t.reshape(shape)
    x = x + _L0_xattn_ref(_layernorm(x, axis=-1), ctx_768, L0_xattn_Wq, L0_xattn_bq, L0_xattn_Wk, L0_xattn_bk, L0_xattn_Wv, L0_xattn_bv, L0_xattn_Wo, L0_xattn_bo)
    x = x + _L0_ffn_ref(_layernorm(x, axis=-1), L0_ffn_norm_scale, L0_ffn_wg, L0_ffn_bg, L0_ffn_w1, L0_ffn_b1, L0_ffn_w2, L0_ffn_b2)
    return x

_drawn_inputs = setup_inputs


def setup_inputs(seed=0):
    import zlib

    import numpy as np

    out = dict(_drawn_inputs(seed))
    spreads = {'L0_ffn_norm_scale': (1.0, 0.6)}
    factors = {'L0_xattn_bq': 8.0,
     'L0_xattn_bk': 64.0,
     'L0_xattn_bv': 6.711,
     'L0_xattn_bo': 5.798,
     'L0_ffn_wg': 8.0,
     'L0_ffn_bg': 8.0,
     'L0_ffn_w1': 8.0,
     'L0_ffn_b1': 8.0,
     'L0_ffn_w2': 8.0,
     'L0_ffn_b2': 23.607}
    for name, (base, spread) in spreads.items():
        noise = np.random.default_rng([zlib.crc32(name.encode()), seed]).standard_normal(out[name].shape)
        drawn = base * np.exp(spread * noise) if base else spread * noise
        out[name] = jnp.asarray(drawn.astype(out[name].dtype))
    for name, factor in factors.items():
        out[name] = (out[name] * factor).astype(out[name].dtype)
    return out
```

```python
import concourse.bass as bass
from concourse import mybir
from contextlib import ExitStack

FP32 = mybir.dt.float32
FP32R = mybir.dt.float32r
BF16 = mybir.dt.bfloat16
U32 = mybir.dt.uint32
ALU = mybir.AluOpType
ACT = mybir.ActivationFunctionType
AX = mybir.AxisListType

B = 2
T = 4
P = 128
N = T * P
D = 128
C = 96
KV = 32
H = 16
HD = D // H
G = 4
HG = H // G
VW = HD + 1
E = 16
I = 128
K = 4
TOP = 8
SCALE = 1.0 / float(HD) ** 0.5
EPS = 1e-5
LIMIT = 7.0
ALPHA = 1.702
GELU_AT_LIMIT = LIMIT / (1.0 + 2.718281828459045 ** (-ALPHA * LIMIT))

PACK = {}
_at = 0
for _name, _n in (("wqT", D), ("woT", D), ("ident", P), ("wg", E), ("head_mask", H), ("group_mask", HG),
                  ("iota", E), ("bq", 1), ("norm_scale", 1)):
    PACK[_name] = (_at, _at + _n)
    _at += _n
PACK_COLS = _at
CTX = {"wkT": (0, D), "wvT": (D, 2 * D), "ctxT": (2 * D, 2 * D + B * KV)}
CTX_COLS = 2 * D + B * KV
W1 = 2 * I
WCOLS = W1 + D + 2


def build(nc, x, pack, ctx, rows, b2, experts, out):
    st = ExitStack()
    with st:
        def sb(name, shape, dt=FP32):
            return st.enter_context(nc.sbuf_tensor(name, shape, dt))

        def sem(name):
            return st.enter_context(nc.semaphore(name))

        x_sb = sb("x_sb", [P, B, T, D])
        pk = sb("pk", [P, PACK_COLS])
        cx = sb("cx", [C + 1, CTX_COLS])
        row_sb = sb("row_sb", [P, D + E])
        b2_sb = sb("b2_sb", [E, D])
        w_sb = sb("w_sb", [P, E * WCOLS])

        def par(name):
            return pk[:, PACK[name][0]:PACK[name][1]]

        def cpar(name):
            return cx[:, CTX[name][0]:CTX[name][1]]
        ident = par("ident")

        half = sb("half", [P, T])
        ctx4 = sb("ctx4", [C + 1, B, G, KV])
        KT = sb("KT", [D, B, KV])
        KBD = sb("KBD", [D, B, H, KV])
        VBD = sb("VBD", [P, B, G, HG, VW])
        xb = sb("xb", [P, B, T, D])
        stats = sb("stats", [P, B, T, 6])
        mv = sb("mv", [P, B, T, 2])
        ve = sb("ve", [P, B, T])
        rstd = sb("rstd", [P, B, T])
        xl = sb("xl", [P, B, T, D])
        xlT = sb("xlT", [D, B, N])
        qT = sb("qT", [D, B, N])
        mx = sb("mx", [P, B, T, H])
        sd = sb("sd", [P, B, T, H * KV])
        pr = sb("pr", [P, B, T, H * KV])
        pT = sb("pT", [P, B, T, G * P])
        rs = sb("rs", [P, B, T, H])
        on = sb("on", [P, B, T, D])
        oT = sb("oT", [D, B, N])
        x1 = sb("x1", [P, B, T, D])
        stats2 = sb("stats2", [P, B, T, 6])
        mv2 = sb("mv2", [P, B, T, 2])
        ve2 = sb("ve2", [P, B, T])
        r1 = sb("r1", [P, B, T])
        msa = sb("msa", [P, B, T])
        msb = sb("msb", [P, B, T])
        msc = sb("msc", [P, B, T])
        r2 = sb("r2", [P, B, T])
        z = sb("z", [P, B, T, D])
        xn = sb("xn", [P, B, T, D])
        base = sb("base", [P, B, T, D])
        baseT = sb("baseT", [D, B, N])
        xnT = sb("xnT", [D, B, N])
        xh = sb("xh", [D, B, N], FP32R)
        xlo = sb("xlo", [D, B, N], FP32R)
        lg = sb("lg", [P, B, T, E])
        top = sb("top", [P, B, T, TOP])
        idx = sb("idx", [P, B, T, TOP], U32)
        idf = sb("idf", [P, B, T, K])
        td = sb("td", [P, B, T, K])
        te = sb("te", [P, B, T, K])
        ts = sb("ts", [P, B, T])
        tr = sb("tr", [P, B, T])
        gk = sb("gk", [P, B, T, K])
        oh = sb("oh", [P, B, T * K, E])
        og = sb("og", [P, B, T * K, E])
        gate = sb("gate", [P, B, T, E])
        gT = sb("gT", [E, B, N])
        ga = sb("ga", [E, B, N])
        gb = sb("gb", [E, B, N], BF16)
        g3 = sb("g3", [96, B, N], BF16)
        sel = sb("sel", [96, E, P], BF16)
        w1h = [sb(f"w1h{s}", [P, W1], FP32R) for s in range(2)]
        w1l = [sb(f"w1l{s}", [P, W1], FP32R) for s in range(2)]
        w2s = [sb(f"w2s{s}", [P, D]) for s in range(2)]
        b1p = sb("b1p", [P, E])
        NS = 4
        ge = [sb(f"ge{s}", [I, N]) for s in range(NS)]
        bt = [sb(f"bt{s}", [I, N]) for s in range(NS)]
        pg = [sb(f"pg{s}", [I, N]) for s in range(NS)]
        sg = [sb(f"sg{s}", [I, N]) for s in range(NS)]
        o_sb = sb("o_sb", [D, B, N])

        bank = [st.enter_context(nc.psum_tensor(f"bank{i}", [P, N], FP32)) for i in range(8)]
        SC = bank[2:6]
        PT = bank[6:8]

        s_pk = sem("s_pk"); s_xin = [sem(f"s_xin{b}") for b in range(B)]; s_cx = sem("s_cx"); s_rw = sem("s_rw"); s_b2 = sem("s_b2")
        s_win = [sem(f"s_win{i}") for i in range(4)]
        s_half = sem("s_half"); s_c4 = sem("s_c4"); s_kv = sem("s_kv"); s_ktb = sem("s_ktb")
        s_kbd = sem("s_kbd"); s_vbd = sem("s_vbd"); s_xb = sem("s_xb"); s_sel = sem("s_sel"); s_g3z = sem("s_g3z")
        s_st = sem("s_st"); s_mv = sem("s_mv"); s_ve = sem("s_ve"); s_rstd = sem("s_rstd"); s_xl = sem("s_xl")
        s_xlTp = sem("s_xlTp"); s_xlT = sem("s_xlT"); s_qp = sem("s_qp"); s_q = sem("s_q")
        s_sc = sem("s_sc"); s_mx = sem("s_mx"); s_sd = sem("s_sd"); s_pr = sem("s_pr")
        s_pTp = sem("s_pTp"); s_pT = sem("s_pT"); s_pv = sem("s_pv"); s_rs = sem("s_rs"); s_on = sem("s_on")
        s_oTp = sem("s_oTp"); s_oT = sem("s_oT"); s_wo = sem("s_wo"); s_x1 = sem("s_x1")
        s_st2 = sem("s_st2"); s_aggr2 = sem("s_aggr2"); s_mv2 = sem("s_mv2"); s_r1 = sem("s_r1"); s_r2 = sem("s_r2"); s_pl = sem("s_pl")
        s_z = sem("s_z"); s_xn = sem("s_xn"); s_base = sem("s_base")
        s_xnTp = sem("s_xnTp"); s_baseTp = sem("s_baseTp"); s_xnT = sem("s_xnT"); s_baseT = sem("s_baseT")
        s_xh = sem("s_xh"); s_xlo = sem("s_xlo"); s_lgp = sem("s_lgp"); s_lg = sem("s_lg")
        s_top = sem("s_top"); s_idx = sem("s_idx"); s_idf = sem("s_idf"); s_td = sem("s_td"); s_te = sem("s_te")
        s_ts = sem("s_ts"); s_tr = sem("s_tr"); s_gk = sem("s_gk"); s_oh = sem("s_oh"); s_og = sem("s_og")
        s_gate = sem("s_gate"); s_gTp = sem("s_gTp"); s_gT = sem("s_gT"); s_g1 = sem("s_g1"); s_ga = sem("s_ga")
        s_gb = sem("s_gb"); s_g2 = sem("s_g2"); s_gc = sem("s_gc")
        s_w1h = sem("s_w1h"); s_w1l = sem("s_w1l"); s_w2 = sem("s_w2"); s_b1p = sem("s_b1p"); s_gp = sem("s_gp"); s_hb = sem("s_hb"); s_ha = sem("s_ha")
        s_ge = sem("s_ge"); s_bt = sem("s_bt"); s_pg = sem("s_pg"); s_sg = sem("s_sg"); s_dn = sem("s_dn")
        s_o = sem("s_o"); s_out = sem("s_out"); s_b2m = sem("s_b2m")

        UNITS = E * B
        block = st.enter_context(nc.Block())

        @block.sync
        def _(sp):
            for b in range(B):
                sp.dma_start(x_sb[:, b], x[b].rearrange("(p t) c -> p t c", t=T)).then_inc(s_xin[b], 16)
                if b == 0:
                    sp.dma_start(pk[:], pack).then_inc(s_pk, 16)
            for i in range(4):
                n = E // 4 * WCOLS
                sp.dma_start(w_sb[:, i * n:(i + 1) * n], experts[:, i * n:(i + 1) * n]).then_inc(s_win[i], 16)
            for b in range(B):
                sp.wait_ge(s_o, b + 1)
                sp.dma_start(out[:, b], o_sb[:, b]).then_inc(s_out, 16)
            sp.wait_ge(s_out, 16 * B)

        @block.gpsimd
        def _(pool):
            nc.gpsimd.memset(half[:], -0.5).then_inc(s_half, 1)
            nc.gpsimd.memset(g3[:], 0.0).then_inc(s_g3z, 1)
            nc.gpsimd.memset(sel[:], 0.0).then_inc(s_g3z, 1)
            pool.wait_ge(s_g3z, 2)
            for j in range(3):
                v = sel[32 * j:32 * j + E, :, :]
                nc.gpsimd.affine_select(out=v, in_=v, compare_op=ALU.not_equal, fill=1.0, base=0,
                                        pattern=[[-1, E], [0, P]], channel_multiplier=1).then_inc(s_sel, 1)
                pool.wait_ge(s_sel, j + 1)

            for b in range(B):
                pool.wait_ge(s_ve, b + 1)
                pool.wait_ge(s_half, 1)
                nc.gpsimd.tensor_tensor(rstd[:, b], ve[:, b], half[:], ALU.pow).then_inc(s_rstd, 1)
            pool.wait_ge(s_rw, 32)
            for b in range(B):
                pool.wait_ge(s_xin[b], 16)
                nc.gpsimd.tensor_tensor(xb[:, b], x_sb[:, b],
                                        row_sb[:, 0:D].unsqueeze(1).to_broadcast([P, T, D]),
                                        ALU.add).then_inc(s_xb, 1)
            for b in range(B):
                pool.wait_ge(s_mv2, b + 1)
                nc.gpsimd.tensor_tensor(r1[:, b], ve2[:, b], half[:], ALU.pow).then_inc(s_r1, 1)
                pool.wait_ge(s_r1, b + 1)
                nc.gpsimd.tensor_tensor(msa[:, b], r1[:, b], r1[:, b], ALU.mult).then_inc(s_pl, 1)
                pool.wait_ge(s_pl, 3 * b + 1)
                nc.gpsimd.tensor_tensor(msb[:, b], msa[:, b], mv2[:, b, :, 1], ALU.mult).then_inc(s_pl, 1)
                pool.wait_ge(s_pl, 3 * b + 2)
                nc.gpsimd.tensor_scalar(msc[:, b], msb[:, b], EPS, None, ALU.add).then_inc(s_pl, 1)
                pool.wait_ge(s_pl, 3 * b + 3)
                nc.gpsimd.tensor_tensor(r2[:, b], msc[:, b], half[:], ALU.pow).then_inc(s_r2, 1)
                pool.wait_ge(s_z, b + 1)
                nc.gpsimd.tensor_tensor(base[:, b], x1[:, b], z[:, b], ALU.add).then_inc(s_base, 1)

        def weights(e):
            return w_sb[:, e * WCOLS:(e + 1) * WCOLS]

        def prepare_w1(dve, e):
            dve.wait_ge(s_win[e // 4], 16)
            if e >= 2:
                dve.wait_ge(s_ha, (e - 1) * B)
            nc.vector.tensor_copy(w1h[e % 2][:], weights(e)[:, 0:W1]).then_inc(s_w1h, 1)
            dve.wait_ge(s_w1h, e + 1)
            nc.vector.tensor_tensor(w1l[e % 2][:], weights(e)[:, 0:W1], w1h[e % 2][:].bitcast(FP32),
                                    ALU.subtract).then_inc(s_w1l, 1)

        def prepare_w2(dve, e):
            if e >= 2:
                dve.wait_ge(s_dn, (e - 1) * B)
            nc.vector.tensor_copy(w2s[e % 2][:], weights(e)[:, W1:W1 + D]).then_inc(s_w2, 1)

        @block.vector
        def _(dve):
            def moments(b):
                dve.wait_ge(s_xin[b], 16)
                for t in range(T):
                    nc.vector.bn_stats(stats[:, b, t], x_sb[:, b, t]).then_inc(s_st, 1)
                for t in range(T):
                    dve.wait_ge(s_st, b * T + t + 1)
                    nc.vector.bn_aggr(mv[:, b, t], stats[:, b, t]).then_inc(s_mv, 1)
                dve.wait_ge(s_mv, T * (b + 1))
                nc.vector.tensor_scalar(ve[:, b], mv[:, b, :, 1], EPS, None, ALU.add).then_inc(s_ve, 1)

            def normalise(b):
                dve.wait_ge(s_rstd, b + 1)
                for t in range(T):
                    nc.vector.tensor_scalar(xl[:, b, t], x_sb[:, b, t], mv[:, b, t, 0:1], rstd[:, b, t:t + 1],
                                            ALU.subtract, ALU.mult).then_inc(s_xl, 1)

            def softmax(b):
                def less(t):
                    dve.wait_ge(s_mx, b * T + t + 1)
                    nc.vector.tensor_tensor(sd[:, b, t].rearrange("p (h k) -> p h k", h=H),
                                            SC[t][:].rearrange("p (h k) -> p h k", h=H),
                                            mx[:, b, t].unsqueeze(2).to_broadcast([P, H, KV]),
                                            ALU.subtract).then_inc(s_sd, 1)
                for t in range(T):
                    dve.wait_ge(s_sc, b * T + t + 1)
                    nc.vector.tensor_reduce(mx[:, b, t], SC[t][:].rearrange("p (h k) -> p h k", h=H),
                                            AX.X, ALU.max).then_inc(s_mx, 1)
                    if t:
                        less(t - 1)
                less(T - 1)

            def divide(b):
                def by(t):
                    dve.wait_ge(s_rs, b * T + t + 1)
                    nc.vector.tensor_tensor(on[:, b, t].rearrange("p (h d) -> p h d", h=H),
                                            SC[t][:, 0:H * VW].rearrange("p (h d) -> p h d", h=H)[:, :, 0:HD],
                                            rs[:, b, t].unsqueeze(2).to_broadcast([P, H, HD]),
                                            ALU.mult).then_inc(s_on, 1)
                for t in range(T):
                    dve.wait_ge(s_pv, b * T + t + 1)
                    nc.vector.reciprocal(rs[:, b, t],
                                         SC[t][:, 0:H * VW].rearrange("p (h d) -> p h d", h=H)[:, :, HD]
                                         ).then_inc(s_rs, 1)
                    if t:
                        by(t - 1)
                by(T - 1)

            def residual(b):
                dve.wait_ge(s_wo, b + 1)
                dve.wait_ge(s_xb, b + 1)
                nc.vector.tensor_tensor(x1[:, b], bank[1][:].rearrange("p (t c) -> p t c", t=T), xb[:, b],
                                        ALU.add).then_inc(s_x1, 1)
                dve.wait_ge(s_x1, b + 1)
                for t in range(T):
                    nc.vector.bn_stats(stats2[:, b, t], x1[:, b, t]).then_inc(s_st2, 1)
                for t in range(T):
                    dve.wait_ge(s_st2, b * T + t + 1)
                    last = nc.vector.bn_aggr(mv2[:, b, t], stats2[:, b, t])
                    last.then_inc(s_aggr2, 1)
                dve.wait_ge(s_aggr2, T * (b + 1))
                nc.vector.tensor_scalar(ve2[:, b], mv2[:, b, :, 1], EPS, None, ALU.add).then_inc(s_mv2, 1)

            def renormalise(b):
                dve.wait_ge(s_r1, b + 1)
                for t in range(T):
                    last = nc.vector.tensor_scalar(z[:, b, t], x1[:, b, t], mv2[:, b, t, 0:1], r1[:, b, t:t + 1],
                                                   ALU.subtract, ALU.mult)
                last.then_inc(s_z, 1)
                dve.wait_ge(s_z, b + 1)
                dve.wait_ge(s_r2, b + 1)
                nc.vector.tensor_tensor(xn[:, b], z[:, b], r2[:, b].unsqueeze(2).to_broadcast([P, T, D]),
                                        ALU.mult).then_inc(s_xn, 1)

            def split_x(b):
                dve.wait_ge(s_xnT, b + 1)
                nc.vector.tensor_copy(xh[:, b], xnT[:, b]).then_inc(s_xh, 1)
                dve.wait_ge(s_xh, b + 1)
                nc.vector.tensor_tensor(xlo[:, b], xnT[:, b], xh[:, b].bitcast(FP32), ALU.subtract).then_inc(s_xlo, 1)

            def route(b):
                dve.wait_ge(s_lgp, b + 1)
                dve.wait_ge(s_rw, 32)
                nc.vector.tensor_tensor(lg[:, b], bank[6][:, 0:T * E].rearrange("p (t e) -> p t e", t=T),
                                        row_sb[:, D:D + E].unsqueeze(1).to_broadcast([P, T, E]),
                                        ALU.add).then_inc(s_lg, 1)
                dve.wait_ge(s_lg, b + 1)
                for t in range(T):
                    nc.vector.max(top[:, b, t], lg[:, b, t]).then_inc(s_top, 1)
                for t in range(T):
                    dve.wait_ge(s_top, b * T + t + 1)
                    nc.vector.max_index(idx[:, b, t], top[:, b, t], lg[:, b, t]).then_inc(s_idx, 1)
                nc.vector.tensor_tensor(td[:, b], top[:, b, :, 0:K], top[:, b, :, 0:1].to_broadcast([P, T, K]),
                                        ALU.subtract).then_inc(s_td, 1)
                dve.wait_ge(s_idx, T * (b + 1))
                nc.vector.tensor_copy(idf[:, b], idx[:, b, :, 0:K]).then_inc(s_idf, 1)
                dve.wait_ge(s_te, b + 1)
                nc.vector.tensor_reduce(ts[:, b], te[:, b], AX.X, ALU.add).then_inc(s_ts, 1)
                dve.wait_ge(s_idf, b + 1)
                nc.vector.tensor_tensor(oh[:, b], par("iota").unsqueeze(1).to_broadcast([P, T * K, E]),
                                        idf[:, b].rearrange("p t k -> p (t k)").unsqueeze(2).to_broadcast([P, T * K, E]),
                                        ALU.is_equal).then_inc(s_oh, 1)
                dve.wait_ge(s_ts, b + 1)
                nc.vector.reciprocal(tr[:, b], ts[:, b]).then_inc(s_tr, 1)
                dve.wait_ge(s_tr, b + 1)
                nc.vector.tensor_tensor(gk[:, b], te[:, b], tr[:, b].unsqueeze(2).to_broadcast([P, T, K]),
                                        ALU.mult).then_inc(s_gk, 1)
                dve.wait_ge(s_gk, b + 1)
                dve.wait_ge(s_oh, b + 1)
                nc.vector.tensor_tensor(og[:, b], oh[:, b],
                                        gk[:, b].rearrange("p t k -> p (t k)").unsqueeze(2).to_broadcast([P, T * K, E]),
                                        ALU.mult).then_inc(s_og, 1)
                dve.wait_ge(s_og, b + 1)
                nc.vector.tensor_reduce(gate[:, b], og[:, b].rearrange("p (t k) e -> p t e k", t=T),
                                        AX.X, ALU.add).then_inc(s_gate, 1)

            def split_gates(b):
                dve.wait_ge(s_gT, b + 1)
                dve.wait_ge(s_g3z, 1)
                nc.vector.tensor_copy(g3[0:E, b], gT[:, b]).then_inc(s_g1, 1)
                dve.wait_ge(s_g1, b + 1)
                nc.vector.tensor_tensor(ga[:, b], gT[:, b], g3[0:E, b], ALU.subtract).then_inc(s_ga, 1)
                dve.wait_ge(s_ga, b + 1)
                nc.vector.tensor_copy(gb[:, b], ga[:, b]).then_inc(s_gb, 1)
                nc.vector.tensor_copy(g3[32:32 + E, b], ga[:, b]).then_inc(s_g2, 1)
                dve.wait_ge(s_gb, b + 1)
                nc.vector.tensor_tensor(g3[64:64 + E, b], ga[:, b], gb[:, b], ALU.subtract).then_inc(s_gc, 1)

            moments(0)
            moments(1)
            normalise(0)
            dve.wait_ge(s_cx, 16)
            nc.vector.tensor_copy(ctx4[:], cpar("ctxT").rearrange("c (b k) -> c b k", b=B).unsqueeze(2)
                                  .to_broadcast([C + 1, B, G, KV])).then_inc(s_c4, 1)
            dve.wait_ge(s_kv, 1)
            nc.vector.tensor_copy(KT[:], bank[6][:, 0:B * KV].rearrange("p (b k) -> p b k", b=B)).then_inc(s_ktb, 1)
            dve.wait_ge(s_ktb, 1)
            dve.wait_ge(s_pk, 16)
            for b in range(B):
                nc.vector.tensor_tensor(KBD[:, b], KT[:, b].unsqueeze(1).to_broadcast([D, H, KV]),
                                        par("head_mask").unsqueeze(2).to_broadcast([D, H, KV]),
                                        ALU.mult).then_inc(s_kbd, 1)
            dve.wait_ge(s_kv, 2)
            for b in range(B):
                for g in range(G):
                    nc.vector.tensor_tensor(
                        VBD[:, b, g, :, 0:HD],
                        bank[7][:, b * D + g * 32:b * D + g * 32 + 32].rearrange("p (j d) -> p j d", d=HD),
                        par("group_mask").unsqueeze(2).to_broadcast([P, HG, HD]), ALU.mult).then_inc(s_vbd, 1)
                    nc.vector.tensor_copy(VBD[:, b, g, :, HD], par("group_mask")).then_inc(s_vbd, 1)
            normalise(1)
            softmax(0)
            divide(0)
            softmax(1)
            residual(0)
            renormalise(0)
            divide(1)
            split_x(0)
            route(0)
            residual(1)
            renormalise(1)
            split_gates(0)
            for e in range(2):
                prepare_w1(dve, e)
                prepare_w2(dve, e)
            for i in range(4):
                dve.wait_ge(s_win[i], 16)
            nc.vector.tensor_scalar(b1p[:], w_sb[:].rearrange("p (e c) -> p e c", e=E)[:, :, WCOLS - 1], 1.0, None,
                                    ALU.add).then_inc(s_b1p, 1)
            split_x(1)
            route(1)
            split_gates(1)

            def upper(u, j):
                dve.wait_ge(s_hb, u + 1)
                if u == 0:
                    dve.wait_ge(s_b1p, 1)
                nc.vector.tensor_scalar(bt[j % NS][:], bank[2 + j % 2][:], b1p[:, u // 2:u // 2 + 1], LIMIT + 1.0,
                                        ALU.add, ALU.min).then_inc(s_bt, 1)

            def gated(u, j):
                dve.wait_ge(s_bt, u + 1)
                dve.wait_ge(s_gp, u + 1)
                nc.vector.scalar_tensor_tensor(pg[j % NS][:], bt[j % NS][:], 1.0 - LIMIT, bank[6 + j % 2][:],
                                               ALU.max, ALU.mult).then_inc(s_pg, 1)

            def product(u, j, first):
                dve.wait_ge(s_ge, u + 1)
                dve.wait_ge(s_pg, u + 1)
                if not first:
                    dve.wait_ge(s_dn, u - NS + 1)
                nc.vector.scalar_tensor_tensor(sg[j % NS][:], ge[j % NS][:], GELU_AT_LIMIT, pg[j % NS][:],
                                               ALU.min, ALU.mult).then_inc(s_sg, 1)

            upper(0, 0)
            gated(0, 0)
            for u in range(UNITS):
                if u + 1 < UNITS:
                    upper(u + 1, u + 1)
                product(u, u, u < NS)
                if u + 1 < UNITS:
                    gated(u + 1, u + 1)
                if u % 2 == 1 and (u + 3) // 2 < E:
                    prepare_w1(dve, (u + 3) // 2)
                if u % 2 == 1 and 2 <= (u + 1) // 2 < E:
                    prepare_w2(dve, (u + 1) // 2)
            for b in range(B):
                dve.wait_ge(s_dn, UNITS - B + b + 1)
                dve.wait_ge(s_baseT, b + 1)
                nc.vector.tensor_tensor(o_sb[:, b], bank[b][:], baseT[:, b], ALU.add).then_inc(s_o, 1)

        @block.scalar
        def _(act):
            act.dma_start(cx[:], ctx).then_inc(s_cx, 16)
            act.dma_start(row_sb[:, 0:D], rows[0:D].partition_broadcast(P)).then_inc(s_rw, 16)
            act.dma_start(row_sb[:, D:D + E], rows[D:D + E].partition_broadcast(P)).then_inc(s_rw, 16)
            act.dma_start(b2_sb[:], b2).then_inc(s_b2, 16)

            def query(b):
                act.wait_ge(s_xlTp, b + 1)
                nc.scalar.copy(xlT[:, b], bank[0][:]).then_inc(s_xlT, 1)
                act.wait_ge(s_qp, b + 1)
                nc.scalar.activation(qT[:, b], bank[1][:], ACT.Identity, bias=par("bq")).then_inc(s_q, 1)

            def probs(b):
                def out_of_psum(t):
                    act.wait_ge(s_pTp, b * T + t + 1)
                    nc.scalar.copy(pT[:, b, t], PT[t % 2][:]).then_inc(s_pT, 1)
                for t in range(T):
                    act.wait_ge(s_sd, b * T + t + 1)
                    nc.scalar.activation(pr[:, b, t], sd[:, b, t], ACT.Exp, scale=SCALE).then_inc(s_pr, 1)
                    if t:
                        out_of_psum(t - 1)
                out_of_psum(T - 1)

            def output(b):
                act.wait_ge(s_oTp, b + 1)
                nc.scalar.copy(oT[:, b], bank[0][:]).then_inc(s_oT, 1)

            def inputs(b):
                act.wait_ge(s_xnTp, b + 1)
                nc.scalar.activation(xnT[:, b], bank[0][:], ACT.Copy, scale=par("norm_scale")).then_inc(s_xnT, 1)
                act.wait_ge(s_baseTp, b + 1)
                nc.scalar.copy(baseT[:, b], bank[1][:]).then_inc(s_baseT, 1)

            def gates(b):
                act.wait_ge(s_td, b + 1)
                nc.scalar.activation(te[:, b], td[:, b], ACT.Exp).then_inc(s_te, 1)
                act.wait_ge(s_gTp, b + 1)
                nc.scalar.copy(gT[:, b], bank[7][0:E, :]).then_inc(s_gT, 1)

            act.wait_ge(s_pk, 16)
            query(0)
            query(1)
            probs(0)
            output(0)
            probs(1)
            inputs(0)
            output(1)
            gates(0)
            inputs(1)
            gates(1)
            for u in range(UNITS):
                e = u // 2
                act.wait_ge(s_ha, u + 1)
                if u % 8 == 0:
                    act.wait_ge(s_win[e // 4], 16)
                if u >= NS:
                    act.wait_ge(s_sg, u - NS + 1)
                nc.scalar.activation(ge[u % NS][:], bank[4 + u % 2][:], ACT.Gelu_apprx_sigmoid,
                                     bias=weights(e)[:, W1 + D:W1 + D + 1]).then_inc(s_ge, 1)

        @block.tensor
        def _(pe):
            def project(b):
                for t in range(T):
                    pe.wait_ge(s_xl, b * T + t + 1)
                    if b and t == 0:
                        pe.wait_ge(s_xlT, b)
                    last = nc.tensor.transpose(bank[0][:, t * P:(t + 1) * P], xl[:, b, t], ident)
                last.then_inc(s_xlTp, 1)
                pe.wait_ge(s_xlT, b + 1)
                if b:
                    pe.wait_ge(s_q, b)
                nc.tensor.matmul(bank[1][:], par("wqT"), xlT[:, b], start=True, stop=True).then_inc(s_qp, 1)

            def scores(b):
                pe.wait_ge(s_q, b + 1)
                pe.wait_ge(s_kbd, b + 1)
                for t in range(T):
                    if b:
                        pe.wait_ge(s_on, (b - 1) * T + t + 1)
                    nc.tensor.matmul(SC[t][:], qT[:, b, t * P:(t + 1) * P], KBD[:, b].rearrange("p h k -> p (h k)"),
                                     start=True, stop=True).then_inc(s_sc, 1)

            def attend(b):
                pe.wait_ge(s_vbd, 2 * G * B)

                def values(t):
                    pe.wait_ge(s_pT, b * T + t + 1)
                    for g in range(G):
                        last = nc.tensor.matmul(SC[t][:, g * HG * VW:(g + 1) * HG * VW],
                                                pT[:, b, t, g * P:(g + 1) * P],
                                                VBD[:, b, g].rearrange("p j d -> p (j d)"), start=True, stop=True)
                    last.then_inc(s_pv, 1)
                for t in range(T):
                    pe.wait_ge(s_pr, b * T + t + 1)
                    if b * T + t >= 2:
                        pe.wait_ge(s_pT, b * T + t - 1)
                    for g in range(G):
                        last = nc.tensor.transpose(PT[t % 2][:, g * P:(g + 1) * P], pr[:, b, t, g * P:(g + 1) * P],
                                                   ident)
                    last.then_inc(s_pTp, 1)
                    if t:
                        values(t - 1)
                values(T - 1)

            def combine(b):
                for t in range(T):
                    pe.wait_ge(s_on, b * T + t + 1)
                    last = nc.tensor.transpose(bank[0][:, t * P:(t + 1) * P], on[:, b, t], ident)
                last.then_inc(s_oTp, 1)
                pe.wait_ge(s_oT, b + 1)
                for t in range(T):
                    last = nc.tensor.matmul(bank[1][:, t * P:(t + 1) * P], oT[:, b, t * P:(t + 1) * P], par("woT"),
                                            start=True, stop=True)
                last.then_inc(s_wo, 1)

            def ffn_inputs(b):
                pe.wait_ge(s_xn, b + 1)
                for t in range(T):
                    last = nc.tensor.transpose(bank[0][:, t * P:(t + 1) * P], xn[:, b, t], ident)
                last.then_inc(s_xnTp, 1)
                pe.wait_ge(s_base, b + 1)
                for t in range(T):
                    last = nc.tensor.transpose(bank[1][:, t * P:(t + 1) * P], base[:, b, t], ident)
                last.then_inc(s_baseTp, 1)
                pe.wait_ge(s_xnT, b + 1)
                if b:
                    pe.wait_ge(s_lg, b)
                for t in range(T):
                    last = nc.tensor.matmul(bank[6][:, t * E:(t + 1) * E], xnT[:, b, t * P:(t + 1) * P], par("wg"),
                                            start=True, stop=True)
                last.then_inc(s_lgp, 1)

            def gates(b):
                pe.wait_ge(s_gate, b + 1)
                if b:
                    pe.wait_ge(s_gT, b)
                for t in range(T):
                    last = nc.tensor.transpose(bank[7][0:E, t * P:(t + 1) * P], gate[:, b, t], ident)
                last.then_inc(s_gTp, 1)

            pe.wait_ge(s_pk, 16)
            pe.wait_ge(s_c4, 1)
            nc.tensor.matmul(bank[6][:, 0:B * KV], cpar("wkT"), cpar("ctxT"), start=True, stop=True).then_inc(s_kv, 1)
            for b in range(B):
                last = nc.tensor.matmul(bank[7][:, b * D:(b + 1) * D], ctx4[:, b].rearrange("c g k -> c (g k)"),
                                        cpar("wvT"), start=True, stop=True)
            last.then_inc(s_kv, 1)
            project(0)
            scores(0)
            project(1)
            attend(0)
            combine(0)
            scores(1)
            attend(1)
            pe.wait_ge(s_x1, 1)
            ffn_inputs(0)
            pe.wait_ge(s_xnT, 1)
            pe.wait_ge(s_baseT, 1)
            combine(1)
            gates(0)
            pe.wait_ge(s_x1, 2)
            pe.wait_ge(s_oT, 2)
            ffn_inputs(1)
            gates(1)

            pe.wait_ge(s_baseT, B)
            pe.wait_ge(s_xnT, B)
            pe.wait_ge(s_b2, 16)
            for b in range(B):
                pe.wait_ge(s_gT, b + 1)
                nc.tensor.matmul(bank[b][:], b2_sb[:], gT[:, b], start=True, stop=False, skip_group_check=True)

            def up(u):
                e, b = u // 2, u % 2
                j = u % 2
                if u < B:
                    pe.wait_ge(s_xlo, b + 1)
                    pe.wait_ge(s_g2, b + 1)
                    pe.wait_ge(s_gc, b + 1)
                    pe.wait_ge(s_sel, 3)
                if b == 0:
                    pe.wait_ge(s_w1l, e + 1)
                for half_, bk, sm, rel in ((1, bank[2 + j], s_hb, s_bt), (0, bank[4 + j], s_ha, s_ge)):
                    cols = slice(half_ * I, (half_ + 1) * I)
                    if u >= 2:
                        pe.wait_ge(rel, u - 1)
                    nc.tensor.matmul(bk[:], w1h[e % 2][:, cols], xh[:, b], start=True, stop=False)
                    nc.tensor.matmul(bk[:], w1h[e % 2][:, cols], xlo[:, b], start=False, stop=False)
                    nc.tensor.matmul(bk[:], w1l[e % 2][:, cols], xh[:, b], start=False, stop=True).then_inc(sm, 1)
                    if half_ == 1:
                        if u >= 2:
                            pe.wait_ge(s_pg, u - 1)
                        nc.tensor.matmul(bank[6 + j][:], sel[:, e], g3[:, b], start=True, stop=True).then_inc(s_gp, 1)

            def down(u):
                e, b = u // 2, u % 2
                pe.wait_ge(s_sg, u + 1)
                if b == 0:
                    pe.wait_ge(s_w2, e + 1)
                nc.tensor.matmul(bank[b][:], w2s[e % 2][:, 0:D], sg[u % NS][:], start=False,
                                 stop=(u >= UNITS - B), skip_group_check=True).then_inc(s_dn, 1)

            for u in range(UNITS + 2):
                if u < UNITS:
                    up(u)
                if u >= 2:
                    down(u - 2)


def kernel(x, ctx_768, L0_xattn_Wq, L0_xattn_bq, L0_xattn_Wk, L0_xattn_bk, L0_xattn_Wv, L0_xattn_bv,
           L0_xattn_Wo, L0_xattn_bo, L0_ffn_norm_scale, L0_ffn_wg, L0_ffn_bg, L0_ffn_w1, L0_ffn_b1,
           L0_ffn_w2, L0_ffn_b2):
    import numpy as np
    import concourse.bacc as bacc
    from concourse.bass_utils import run_bass_kernel_spmd

    a = [np.asarray(v) for v in (x, ctx_768, L0_xattn_Wq, L0_xattn_bq, L0_xattn_Wk, L0_xattn_bk, L0_xattn_Wv,
                                 L0_xattn_bv, L0_xattn_Wo, L0_xattn_bo, L0_ffn_norm_scale, L0_ffn_wg, L0_ffn_bg,
                                 L0_ffn_w1, L0_ffn_b1, L0_ffn_w2, L0_ffn_b2)]
    x, ctx, wq, bq, wk, bk, wv, bv, wo, bo, ns, wg, bg, w1, b1, w2, b2 = a
    f = np.float32
    p = np.arange(P)
    ident = np.eye(P, dtype=f)
    head_mask = (p[:, None] // HD == np.arange(H)[None]).astype(f)
    group_mask = (p[:, None] // KV == np.arange(HG)[None]).astype(f)
    iota = np.broadcast_to(np.arange(E, dtype=f), (P, E))
    pack = np.concatenate([wq.T, wo.T, ident, wg, head_mask, group_mask, iota, bq[:, None], ns[:, None]], axis=1)
    ctx_pack = np.concatenate([
        np.concatenate([wk.T, bk[None]], axis=0),
        np.concatenate([wv.T, bv[None]], axis=0),
        np.concatenate([ctx.reshape(B * KV, C).T, np.ones((1, B * KV), f)], axis=0)], axis=1)
    w1s = w1.reshape(E, D, I, 2).transpose(1, 0, 3, 2).reshape(D, E, 2 * I)
    b1s = b1.reshape(E, I, 2).transpose(1, 0, 2)
    experts = np.concatenate([w1s, w2.transpose(1, 0, 2), b1s], axis=2).reshape(P, E * WCOLS)
    rows = np.concatenate([bo, bg])
    arrays = {"x": x, "pack": pack, "ctx": ctx_pack, "rows": rows, "b2": b2, "experts": experts}
    arrays = {k: np.ascontiguousarray(v) for k, v in arrays.items()}
    nc = bacc.Bacc("TRN2", target_bir_lowering=False, num_devices=1)
    args = [nc.dram_tensor(f"in_{k}", v.shape, mybir.dt.from_np(v.dtype), kind="ExternalInput").ap()
            for k, v in arrays.items()]
    out = nc.dram_tensor("out", (D, B, N), FP32, kind="ExternalOutput").ap()
    build(nc, *args, out)
    r = run_bass_kernel_spmd(nc, [{f"in_{k}": v for k, v in arrays.items()}], core_ids=[0])
    got = r.results[0]["out"]
    return np.ascontiguousarray(got.reshape(D, B, T, P).transpose(1, 3, 2, 0).reshape(B, N, D))
```

```python
import concourse.bass as bass
from concourse import mybir
from contextlib import ExitStack

FP32 = mybir.dt.float32
FP32R = mybir.dt.float32r
BF16 = mybir.dt.bfloat16
U32 = mybir.dt.uint32
ALU = mybir.AluOpType
ACT = mybir.ActivationFunctionType
AX = mybir.AxisListType

B = 2
T = 4
P = 128
N = T * P
D = 128
C = 96
KV = 32
H = 16
HD = D // H
G = 4
HG = H // G
VW = HD + 1
E = 16
I = 128
K = 4
LAG = 4
TOP = 8
SCALE = 1.0 / float(HD) ** 0.5
EPS = 1e-5
LIMIT = 7.0
ALPHA = 1.702
GELU_AT_LIMIT = LIMIT / (1.0 + 2.718281828459045 ** (-ALPHA * LIMIT))

PACK = {}
_at = 0
for _name, _n in (("wqT", D), ("woT", D), ("ident", P), ("wg", E), ("head_mask", H), ("group_mask", HG),
                  ("iota", E), ("bq", 1), ("norm_scale", 1)):
    PACK[_name] = (_at, _at + _n)
    _at += _n
PACK_COLS = _at
CTX = {"wkT": (0, D), "wvT": (D, 2 * D), "ctxT": (2 * D, 2 * D + B * KV)}
CTX_COLS = 2 * D + B * KV
W1 = 2 * I
Q = 4
QUADS = E // Q


def build(nc, x, pack, ctx, rows, b2, w1, w2, b1, out):
    gate_rows = nc.dram_tensor("gate_rows", (E, B, N), FP32).ap()
    st = ExitStack()
    with st:
        def sb(name, shape, dt=FP32):
            return st.enter_context(nc.sbuf_tensor(name, shape, dt))

        def sem(name):
            return st.enter_context(nc.semaphore(name))

        x_sb = sb("x_sb", [P, B, T, D])
        pk = sb("pk", [P, PACK_COLS])
        cx = sb("cx", [C + 1, CTX_COLS])
        row_sb = sb("row_sb", [P, D + E])
        b2_sb = sb("b2_sb", [E, D])
        w1_sb = sb("w1_sb", [D, E * W1])
        b1_sb = sb("b1_sb", [I, 2 * E])
        b1p = sb("b1p", [I, E])

        def par(name):
            return pk[:, PACK[name][0]:PACK[name][1]]

        def cpar(name):
            return cx[:, CTX[name][0]:CTX[name][1]]
        ident = par("ident")
        half = sb("half", [P, T])
        ctx4 = sb("ctx4", [C + 1, B, G, KV])
        KT = sb("KT", [D, B, KV])
        KBD = sb("KBD", [D, B, H, KV])
        VBD = sb("VBD", [P, B, G, HG, VW])
        xb = sb("xb", [P, B, T, D])
        stats = sb("stats", [P, B, T, 6])
        mv = sb("mv", [P, B, T, 2])
        ve = sb("ve", [P, B, T])
        rstd = sb("rstd", [P, B, T])
        xl = sb("xl", [P, B, T, D])
        xlT = sb("xlT", [D, B, N])
        qT = sb("qT", [D, B, N])
        mx = sb("mx", [P, B, T, H])
        sd = sb("sd", [P, B, T, H * KV])
        pr = sb("pr", [P, B, T, H * KV])
        pT = sb("pT", [P, B, T, G * P])
        rs = sb("rs", [P, B, T, H])
        on = sb("on", [P, B, T, D])
        oT = sb("oT", [D, B, N])
        x1 = sb("x1", [P, B, T, D])
        stats2 = sb("stats2", [P, B, T, 6])
        mv2 = sb("mv2", [P, B, T, 2])
        v2a = sb("v2a", [P, B, T])
        v2b = sb("v2b", [P, B, T])
        r12 = sb("r12", [P, B, T])
        r1 = sb("r1", [P, B, T])
        r1p = sb("r1p", [P, B, T])
        mr = sb("mr", [P, B, T])
        nmr = sb("nmr", [P, B, T])
        xn = sb("xn", [P, B, T, D])
        base = sb("base", [P, B, T, D])
        baseT = sb("baseT", [D, B, N])
        xh = sb("xh", [D, B, N], FP32R)
        xlo = sb("xlo", [D, B, N], FP32R)
        wgh = sb("wgh", [D, E], FP32R)
        wgl = sb("wgl", [D, E], FP32R)
        lg = sb("lg", [P, B, T, E])
        top = sb("top", [P, B, T, TOP])
        idx = sb("idx", [P, B, T, TOP], U32)
        idf = sb("idf", [P, B, T, K])
        td = sb("td", [P, B, T, K])
        te = sb("te", [P, B, T, K])
        ts = sb("ts", [P, B, T])
        tr = sb("tr", [P, B, T])
        gk = sb("gk", [P, B, T, K])
        oh = sb("oh", [P, B, T * K, E])
        og = sb("og", [P, B, T * K, E])
        gate = sb("gate", [P, B, T, E])
        gT = sb("gT", [E, B, N])
        w1h = [sb(f"w1h{s}", [D, W1], FP32R) for s in range(Q)]
        w1l = [sb(f"w1l{s}", [D, W1], FP32R) for s in range(Q)]
        w2s = [sb(f"w2s{s}", [I, D]) for s in range(Q)]
        gates_sb = [[sb(f"gates{b}{s}", [P, N]) for s in range(Q)] for b in range(B)]
        NS = 4
        ge = [sb(f"ge{s}", [I, N]) for s in range(NS)]
        bt = [sb(f"bt{s}", [I, N]) for s in range(NS)]
        pg = [sb(f"pg{s}", [I, N]) for s in range(NS)]
        sg = [sb(f"sg{s}", [I, N]) for s in range(NS)]
        o_sb = sb("o_sb", [D, B, N])
        warm = sb("warm", [P, N], BF16)

        bank = [st.enter_context(nc.psum_tensor(f"bank{i}", [P, N], FP32)) for i in range(8)]
        XT, QW = bank[0], bank[1]
        SC = bank[2:6]
        PT = bank[6:8]
        XNT = [bank[2], bank[7]]
        LGP = [bank[3], bank[6]]
        GTP = [bank[6], bank[6]]
        BST = [bank[6], bank[7]]
        ACC = bank[0:2]
        HB = bank[2:4]
        HA = bank[4:6]

        pk_in = sem("pk_in")
        x_in = [sem(f"x_in{b}") for b in range(B)]
        ctx_in = sem("ctx_in")
        rows_in = sem("rows_in")
        b1_in = sem("b1_in")
        b2_in = sem("b2_in")
        w1_in = [sem(f"w1_in{q}") for q in range(QUADS)]
        w2_in = [sem(f"w2_in{s}") for s in range(Q)]
        gates_in = [[sem(f"gates_in{b}{s}") for s in range(Q)] for b in range(B)]
        half_set = sem("half_set"); warm_set = sem("warm_set")
        ctx4_made = sem("ctx4_made"); kv_psum = sem("kv_psum"); kt_made = sem("kt_made")
        kbd_made = sem("kbd_made"); vbd_made = sem("vbd_made"); xb_made = sem("xb_made")
        stats_made = sem("stats_made"); mv_made = sem("mv_made"); ve_made = sem("ve_made")
        rstd_made = sem("rstd_made"); xl_made = sem("xl_made"); xlT_psum = sem("xlT_psum")
        xlT_made = sem("xlT_made"); q_psum = sem("q_psum"); q_made = sem("q_made")
        scores_psum = sem("scores_psum"); mx_made = sem("mx_made"); sd_made = sem("sd_made")
        pr_made = sem("pr_made"); pT_psum = sem("pT_psum"); pT_made = sem("pT_made"); pv_psum = sem("pv_psum")
        rs_made = sem("rs_made"); on_made = sem("on_made"); oT_psum = sem("oT_psum"); oT_made = sem("oT_made")
        wo_psum = sem("wo_psum"); x1_made = sem("x1_made"); stats2_made = sem("stats2_made")
        mv2_made = sem("mv2_made"); v2a_made = sem("v2a_made"); v2b_made = sem("v2b_made")
        r12_made = sem("r12_made"); r1_made = sem("r1_made"); mr_made = sem("mr_made"); nmr_made = sem("nmr_made")
        xn_made = sem("xn_made"); base_made = sem("base_made"); xnT_psum = sem("xnT_psum")
        baseT_psum = sem("baseT_psum"); baseT_made = sem("baseT_made")
        wgh_made = sem("wgh_made"); wgl_made = sem("wgl_made"); xh_made = sem("xh_made"); xlo_made = sem("xlo_made")
        lg_psum = sem("lg_psum"); lg_made = sem("lg_made"); top_made = sem("top_made"); idx_made = sem("idx_made")
        idf_made = sem("idf_made"); td_made = sem("td_made"); te_made = sem("te_made"); ts_made = sem("ts_made")
        tr_made = sem("tr_made"); gk_made = sem("gk_made"); oh_made = sem("oh_made"); og_made = sem("og_made")
        gate_made = sem("gate_made"); gT_psum = sem("gT_psum"); gT_made = sem("gT_made")
        gates_out = [sem(f"gates_out{b}") for b in range(B)]
        b1p_made = sem("b1p_made")
        first_w1h = sem("first_w1h"); first_w1l = sem("first_w1l")
        w1h_made = sem("w1h_made"); w1l_made = sem("w1l_made")
        hb_psum = sem("hb_psum"); ha_psum = sem("ha_psum")
        ge_made = sem("ge_made"); bt_made = sem("bt_made"); pg_made = sem("pg_made"); sg_made = sem("sg_made")
        down_done = sem("down_done"); o_made = sem("o_made")
        out_done = [sem(f"out_done{b}") for b in range(B)]

        def raw_w1(e):
            return w1_sb[:, bass.ds(e * W1, W1)]

        block = st.enter_context(nc.Block())

        @block.sync
        def _(sp):
            sp.dma_start(x_sb[:, 0], x[0].rearrange("(p t) c -> p t c", t=T)).then_inc(x_in[0], 16)
            sp.dma_start(x_sb[:, 1], x[1].rearrange("(p t) c -> p t c", t=T)).then_inc(x_in[1], 16)
            sp.dma_start(row_sb[:, 0:D], rows[0:D].partition_broadcast(P)).then_inc(rows_in, 16)
            sp.dma_start(row_sb[:, D:D + E], rows[D:D + E].partition_broadcast(P)).then_inc(rows_in, 16)
            for q in range(QUADS):
                sp.dma_start(w1_sb[:, q * Q * W1:(q + 1) * Q * W1],
                             w1[:, q * Q * W1:(q + 1) * Q * W1]).then_inc(w1_in[q], 16)
                if q == 0:
                    for s in range(Q):
                        sp.dma_start(w2s[s][:], w2[s]).then_inc(w2_in[s], 16)
                    sp.dma_start(b1_sb[:], b1).then_inc(b1_in, 16)
                    sp.dma_start(b2_sb[:], b2).then_inc(b2_in, 16)
            for b in range(B):
                sp.wait_ge(gT_made, b + 1)
                sp.dma_start(gate_rows[:, b], gT[:, b]).then_inc(gates_out[b], 16)
                sp.wait_ge(gates_out[b], 16)
                for s in range(Q):
                    sp.dma_start(gates_sb[b][s][:], gate_rows[s, b].partition_broadcast(P)
                                 ).then_inc(gates_in[b][s], 16)
            with sp.Fori(0, QUADS - 1) as q:
                for b in range(B):
                    for s in range(Q):
                        sp.wait_ge(pg_made, q * (B * Q) + (b * Q + s + 1))
                        sp.dma_start(gates_sb[b][s][:],
                                     gate_rows[bass.ds(q * Q + (Q + s), 1), b].partition_broadcast(P)
                                     ).then_inc(gates_in[b][s], 16)
                        if b == B - 1:
                            sp.wait_ge(down_done, q * (B * Q) + (b * Q + s + 1))
                            sp.dma_start(w2s[s][:], w2[bass.ds(q * Q + (Q + s), 1)].rearrange("a i d -> (a i) d")
                                         ).then_inc(w2_in[s], 16)
            for b in range(B):
                sp.wait_ge(o_made, b + 1)
                sp.dma_start(out[:, b], o_sb[:, b]).then_inc(out_done[b], 16)
            for b in range(B):
                sp.wait_ge(out_done[b], 16)

        @block.gpsimd
        def _(pool):
            nc.gpsimd.memset(half[:], -0.5).then_inc(half_set, 1)
            pool.wait_ge(half_set, 1)
            for b in range(B):
                pool.wait_ge(ve_made, b + 1)
                nc.gpsimd.tensor_tensor(rstd[:, b], ve[:, b], half[:], ALU.pow).then_inc(rstd_made, 1)
            pool.wait_ge(rows_in, 32)
            for b in range(B):
                pool.wait_ge(x_in[b], 16)
                nc.gpsimd.tensor_tensor(xb[:, b], x_sb[:, b],
                                        row_sb[:, 0:D].unsqueeze(1).to_broadcast([P, T, D]),
                                        ALU.add).then_inc(xb_made, 1)
            pool.wait_ge(pk_in, 16)
            nc.gpsimd.tensor_copy(wgh[:], par("wg")).then_inc(wgh_made, 1)
            pool.wait_ge(wgh_made, 1)
            nc.gpsimd.tensor_tensor(wgl[:], par("wg"), wgh[:].bitcast(FP32), ALU.subtract).then_inc(wgl_made, 1)
            pool.wait_ge(w1_in[0], 16)
            for s in range(Q):
                nc.gpsimd.tensor_copy(w1h[s][:], raw_w1(s)).then_inc(first_w1h, 1)
                pool.wait_ge(first_w1h, s + 1)
                nc.gpsimd.tensor_tensor(w1l[s][:], raw_w1(s), w1h[s][:].bitcast(FP32),
                                        ALU.subtract).then_inc(first_w1l, 1)
            pool.wait_ge(b1_in, 16)
            nc.gpsimd.tensor_scalar(b1p[:], b1_sb[:, E:2 * E], 1.0, None, ALU.add).then_inc(b1p_made, 1)
            for b in range(B):
                pool.wait_ge(v2b_made, b + 1)
                nc.gpsimd.tensor_tensor(r12[:, b], v2b[:, b], half[:], ALU.pow).then_inc(r12_made, 1)
                pool.wait_ge(v2a_made, b + 1)
                nc.gpsimd.tensor_tensor(r1[:, b], v2a[:, b], half[:], ALU.pow).then_inc(r1_made, 1)
                pool.wait_ge(r1_made, b + 1)
                nc.gpsimd.tensor_tensor(mr[:, b], mv2[:, b, :, 0], r1[:, b], ALU.mult).then_inc(mr_made, 1)
                nc.gpsimd.tensor_scalar(r1p[:, b], r1[:, b], 1.0, None, ALU.add).then_inc(nmr_made, 1)
                pool.wait_ge(mr_made, b + 1)
                nc.gpsimd.tensor_scalar(nmr[:, b], mr[:, b], -1.0, None, ALU.mult).then_inc(nmr_made, 1)

        @block.vector
        def _(dve):
            def moments(b):
                dve.wait_ge(x_in[b], 16)
                for t in range(T):
                    nc.vector.bn_stats(stats[:, b, t], x_sb[:, b, t]).then_inc(stats_made, 1)
                for t in range(T):
                    dve.wait_ge(stats_made, b * T + t + 1)
                    nc.vector.bn_aggr(mv[:, b, t], stats[:, b, t]).then_inc(mv_made, 1)
                dve.wait_ge(mv_made, T * (b + 1))
                nc.vector.tensor_scalar(ve[:, b], mv[:, b, :, 1], EPS, None, ALU.add).then_inc(ve_made, 1)

            def normalise(b):
                dve.wait_ge(rstd_made, b + 1)
                for t in range(T):
                    nc.vector.tensor_scalar(xl[:, b, t], x_sb[:, b, t], mv[:, b, t, 0:1], rstd[:, b, t:t + 1],
                                            ALU.subtract, ALU.mult).then_inc(xl_made, 1)

            def maximum(n):
                dve.wait_ge(scores_psum, n + 1)
                nc.vector.tensor_reduce(mx[:, n // T, n % T], SC[n % T][:].rearrange("p (h k) -> p h k", h=H),
                                        AX.X, ALU.max).then_inc(mx_made, 1)

            def less_maximum(n):
                dve.wait_ge(mx_made, n + 1)
                nc.vector.tensor_tensor(sd[:, n // T, n % T].rearrange("p (h k) -> p h k", h=H),
                                        SC[n % T][:].rearrange("p (h k) -> p h k", h=H),
                                        mx[:, n // T, n % T].unsqueeze(2).to_broadcast([P, H, KV]),
                                        ALU.subtract).then_inc(sd_made, 1)

            def one_over_sum(n):
                dve.wait_ge(pv_psum, n + 1)
                nc.vector.reciprocal(rs[:, n // T, n % T],
                                     PT[n % 2][:, 0:H * VW].rearrange("p (h d) -> p h d", h=H)[:, :, HD]
                                     ).then_inc(rs_made, 1)

            def divide(n):
                dve.wait_ge(rs_made, n + 1)
                nc.vector.tensor_tensor(on[:, n // T, n % T].rearrange("p (h d) -> p h d", h=H),
                                        PT[n % 2][:, 0:H * VW].rearrange("p (h d) -> p h d", h=H)[:, :, 0:HD],
                                        rs[:, n // T, n % T].unsqueeze(2).to_broadcast([P, H, HD]),
                                        ALU.mult).then_inc(on_made, 1)

            def residual(b):
                dve.wait_ge(wo_psum, b + 1)
                dve.wait_ge(xb_made, b + 1)
                nc.vector.tensor_tensor(x1[:, b], QW[:].rearrange("p (t c) -> p t c", t=T), xb[:, b],
                                        ALU.add).then_inc(x1_made, 1)
                dve.wait_ge(x1_made, b + 1)
                for t in range(T):
                    nc.vector.bn_stats(stats2[:, b, t], x1[:, b, t]).then_inc(stats2_made, 1)
                for t in range(T):
                    dve.wait_ge(stats2_made, b * T + t + 1)
                    nc.vector.bn_aggr(mv2[:, b, t], stats2[:, b, t]).then_inc(mv2_made, 1)
                dve.wait_ge(mv2_made, T * (b + 1))
                nc.vector.tensor_scalar(v2b[:, b], mv2[:, b, :, 1], 1.0 + EPS, EPS * EPS, ALU.mult,
                                        ALU.add).then_inc(v2b_made, 1)
                nc.vector.tensor_scalar(v2a[:, b], mv2[:, b, :, 1], EPS, None, ALU.add).then_inc(v2a_made, 1)

            def renormalise(b):
                dve.wait_ge(r12_made, b + 1)
                for t in range(T):
                    nc.vector.tensor_scalar(xn[:, b, t], x1[:, b, t], mv2[:, b, t, 0:1], r12[:, b, t:t + 1],
                                            ALU.subtract, ALU.mult).then_inc(xn_made, 1)

            def low_part(b):
                dve.wait_ge(xh_made, b + 1)
                nc.vector.scalar_tensor_tensor(xlo[:, b], XNT[b][:], par("norm_scale"), xh[:, b].bitcast(FP32),
                                               ALU.mult, ALU.subtract).then_inc(xlo_made, 1)

            def choose(b):
                dve.wait_ge(lg_psum, b + 1)
                nc.vector.tensor_tensor(lg[:, b], LGP[b][:, 0:T * E].rearrange("p (t e) -> p t e", t=T),
                                        row_sb[:, D:D + E].unsqueeze(1).to_broadcast([P, T, E]),
                                        ALU.add).then_inc(lg_made, 1)
                dve.wait_ge(lg_made, b + 1)
                for t in range(T):
                    nc.vector.max(top[:, b, t], lg[:, b, t]).then_inc(top_made, 1)
                dve.wait_ge(top_made, T * (b + 1))
                nc.vector.tensor_tensor(td[:, b], top[:, b, :, 0:K], top[:, b, :, 0:1].to_broadcast([P, T, K]),
                                        ALU.subtract).then_inc(td_made, 1)
                for t in range(T):
                    nc.vector.max_index(idx[:, b, t], top[:, b, t], lg[:, b, t]).then_inc(idx_made, 1)
                dve.wait_ge(idx_made, T * (b + 1))
                nc.vector.tensor_copy(idf[:, b], idx[:, b, :, 0:K]).then_inc(idf_made, 1)

            def weigh(b):
                dve.wait_ge(te_made, b + 1)
                nc.vector.tensor_reduce(ts[:, b], te[:, b], AX.X, ALU.add).then_inc(ts_made, 1)
                dve.wait_ge(idf_made, b + 1)
                nc.vector.tensor_tensor(oh[:, b], par("iota").unsqueeze(1).to_broadcast([P, T * K, E]),
                                        idf[:, b].rearrange("p t k -> p (t k)").unsqueeze(2)
                                        .to_broadcast([P, T * K, E]), ALU.is_equal).then_inc(oh_made, 1)
                dve.wait_ge(ts_made, b + 1)
                nc.vector.reciprocal(tr[:, b], ts[:, b]).then_inc(tr_made, 1)
                dve.wait_ge(tr_made, b + 1)
                nc.vector.tensor_tensor(gk[:, b], te[:, b], tr[:, b].unsqueeze(2).to_broadcast([P, T, K]),
                                        ALU.mult).then_inc(gk_made, 1)
                dve.wait_ge(gk_made, b + 1)
                dve.wait_ge(oh_made, b + 1)
                nc.vector.tensor_tensor(og[:, b], oh[:, b],
                                        gk[:, b].rearrange("p t k -> p (t k)").unsqueeze(2)
                                        .to_broadcast([P, T * K, E]), ALU.mult).then_inc(og_made, 1)
                dve.wait_ge(og_made, b + 1)
                nc.vector.tensor_reduce(gate[:, b], og[:, b].rearrange("p (t k) e -> p t e k", t=T),
                                        AX.X, ALU.add).then_inc(gate_made, 1)

            def upper(n, j, e):
                dve.wait_ge(hb_psum, n + 1)
                nc.vector.tensor_scalar(bt[j % NS][:], HB[j % 2][:], b1p[:, bass.ds(e, 1)], LIMIT + 1.0,
                                        ALU.add, ALU.min).then_inc(bt_made, 1)

            def gated(n, j, q):
                dve.wait_ge(bt_made, n + 1)
                dve.wait_ge(gates_in[j // Q][j % Q], q * 16 + 16)
                nc.vector.scalar_tensor_tensor(pg[j % NS][:], bt[j % NS][:], 1.0 - LIMIT, gates_sb[j // Q][j % Q][:],
                                               ALU.max, ALU.mult).then_inc(pg_made, 1)

            def product(n, j):
                dve.wait_ge(ge_made, n + 1)
                dve.wait_ge(pg_made, n + 1)
                nc.vector.scalar_tensor_tensor(sg[j % NS][:], ge[j % NS][:], GELU_AT_LIMIT, pg[j % NS][:],
                                               ALU.min, ALU.mult).then_inc(sg_made, 1)

            nc.vector.memset(warm[:], 0.0).then_inc(warm_set, 1)
            moments(0)
            dve.wait_ge(ctx_in, 16)
            nc.vector.tensor_copy(ctx4[:], cpar("ctxT").rearrange("c (b k) -> c b k", b=B).unsqueeze(2)
                                  .to_broadcast([C + 1, B, G, KV])).then_inc(ctx4_made, 1)
            normalise(0)
            moments(1)
            dve.wait_ge(kv_psum, 1)
            nc.vector.tensor_copy(KT[:], PT[0][:, 0:B * KV].rearrange("p (b k) -> p b k", b=B)).then_inc(kt_made, 1)
            dve.wait_ge(kt_made, 1)
            dve.wait_ge(pk_in, 16)
            for b in range(B):
                nc.vector.tensor_tensor(KBD[:, b], KT[:, b].unsqueeze(1).to_broadcast([D, H, KV]),
                                        par("head_mask").unsqueeze(2).to_broadcast([D, H, KV]),
                                        ALU.mult).then_inc(kbd_made, 1)
            normalise(1)
            dve.wait_ge(kv_psum, 2)
            for b in range(B):
                for g in range(G):
                    nc.vector.tensor_tensor(
                        VBD[:, b, g, :, 0:HD],
                        PT[1][:, b * D + g * 32:b * D + g * 32 + 32].rearrange("p (j d) -> p j d", d=HD),
                        par("group_mask").unsqueeze(2).to_broadcast([P, HG, HD]), ALU.mult).then_inc(vbd_made, 1)
                nc.vector.tensor_copy(VBD[:, b, :, :, HD], par("group_mask").unsqueeze(1)
                                      .to_broadcast([P, G, HG])).then_inc(vbd_made, 1)
            for n in range(B * T + LAG):
                if n >= LAG:
                    one_over_sum(n - LAG)
                if 1 <= n <= B * T:
                    less_maximum(n - 1)
                if n >= LAG:
                    divide(n - LAG)
                if n < B * T:
                    maximum(n)
                if n == T + LAG + 1:
                    residual(0)
            dve.wait_ge(rows_in, 32)
            renormalise(0)
            residual(1)
            low_part(0)
            choose(0)
            renormalise(1)
            weigh(0)

            dve.wait_ge(b1p_made, 1)
            low_part(1)
            upper(0, 0, 0)
            upper(1, 1, 1)
            choose(1)
            gated(0, 0, 0)
            gated(1, 1, 0)
            product(0, 0)
            weigh(1)
            for j in (2, 3):
                upper(j, j, j)
                product(j - 1, j - 1)
                gated(j, j, 0)

            def step(q, k):
                n, j = q * (B * Q) + (Q + k), (Q + k) % (B * Q)
                later = k // Q
                upper(n, j, q * Q + (Q * later + j % Q))
                product(n - 1, (j - 1) % (B * Q))
                gated(n, j, q + later)

            with dve.Fori(0, QUADS - 1) as q:
                for k in range(B * Q):
                    step(q, k)
                    if 1 <= k <= Q:
                        s = k - 1
                        dve.wait_ge(w1h_made, q * Q + (s + 1))
                        nc.vector.tensor_tensor(w1l[s][:], raw_w1(q * Q + (Q + s)), w1h[s][:].bitcast(FP32),
                                                ALU.subtract).then_inc(w1l_made, 1)
            for k in range(Q):
                step(QUADS - 1, k)
            product(B * E - 1, B * Q - 1)
            for b in range(B):
                dve.wait_ge(down_done, B * E - Q * (B - 1 - b))
                dve.wait_ge(baseT_made, B)
                nc.vector.tensor_tensor(o_sb[:, b], ACC[b][:], baseT[:, b], ALU.add).then_inc(o_made, 1)

        @block.scalar
        def _(act):
            act.dma_start(cx[:], ctx).then_inc(ctx_in, 16)
            act.dma_start(pk[:], pack).then_inc(pk_in, 16)
            nc.scalar.preload_act_table(ACT.Exp)

            def query(b):
                act.wait_ge(xlT_psum, b + 1)
                nc.scalar.copy(xlT[:, b], XT[:]).then_inc(xlT_made, 1)
                act.wait_ge(q_psum, b + 1)
                nc.scalar.activation(qT[:, b], QW[:], ACT.Identity, bias=par("bq")).then_inc(q_made, 1)

            def exponential(n):
                act.wait_ge(sd_made, n + 1)
                nc.scalar.activation(pr[:, n // T, n % T], sd[:, n // T, n % T], ACT.Exp,
                                     scale=SCALE).then_inc(pr_made, 1)

            def out_of_psum(n):
                act.wait_ge(pT_psum, n + 1)
                nc.scalar.copy(pT[:, n // T, n % T], PT[n % 2][:]).then_inc(pT_made, 1)

            def output(b):
                act.wait_ge(oT_psum, b + 1)
                nc.scalar.copy(oT[:, b], XT[:]).then_inc(oT_made, 1)

            def bases(b):
                act.wait_ge(nmr_made, 2 * (b + 1))
                for t in range(T):
                    nc.scalar.activation(base[:, b, t], x1[:, b, t], ACT.Identity, bias=nmr[:, b, t:t + 1],
                                         scale=r1p[:, b, t:t + 1]).then_inc(base_made, 1)

            def high_part(b):
                act.wait_ge(xnT_psum, b + 1)
                nc.scalar.activation(xh[:, b], XNT[b][:], ACT.Copy, scale=par("norm_scale")).then_inc(xh_made, 1)

            def base_out(b):
                act.wait_ge(baseT_psum, B - b)
                nc.scalar.copy(baseT[:, b], BST[b][:]).then_inc(baseT_made, 1)

            def choice(b):
                act.wait_ge(td_made, b + 1)
                nc.scalar.activation(te[:, b], td[:, b], ACT.Exp).then_inc(te_made, 1)

            def gates(b):
                act.wait_ge(gT_psum, b + 1)
                nc.scalar.copy(gT[:, b], GTP[b][0:E, :]).then_inc(gT_made, 1)

            def activate(n, j, e):
                act.wait_ge(ha_psum, n + 1)
                nc.scalar.activation(ge[j % NS][:], HA[j % 2][:], ACT.Gelu_apprx_sigmoid,
                                     bias=b1_sb[:, bass.ds(e, 1)]).then_inc(ge_made, 1)

            act.wait_ge(pk_in, 16)
            query(0)
            query(1)
            for n in range(B * T + 1):
                if n < B * T:
                    exponential(n)
                if n:
                    out_of_psum(n - 1)
                if n == B * T - 1:
                    output(0)
            output(1)
            high_part(0)
            choice(0)
            bases(0)
            high_part(1)
            gates(0)
            act.wait_ge(b1_in, 16)
            activate(0, 0, 0)
            activate(1, 1, 1)
            choice(1)
            bases(1)
            activate(2, 2, 2)
            gates(1)
            activate(3, 3, 3)
            base_out(1)
            base_out(0)

            def step(q, k):
                n, j = q * (B * Q) + (Q + k), (Q + k) % (B * Q)
                activate(n, j, q * Q + (Q * (k // Q) + j % Q))

            for q in range(1, QUADS):
                act.wait_ge(w1_in[q], 16)
            with act.Fori(0, QUADS - 1) as q:
                for k in range(B * Q):
                    step(q, k)
                    if k < Q:
                        nc.scalar.copy(w1h[k][:], raw_w1(q * Q + (Q + k))).then_inc(w1h_made, 1)
            for k in range(Q):
                step(QUADS - 1, k)

        @block.tensor
        def _(pe):
            def warm_up(count):
                for _ in range(count):
                    nc.tensor.matmul(SC[0][:], warm[:, 0:P], warm[:], start=True, stop=True)

            def project(b):
                for t in range(T):
                    pe.wait_ge(xl_made, b * T + t + 1)
                    if b and t == 0:
                        pe.wait_ge(xlT_made, b)
                    last = nc.tensor.transpose(XT[:, t * P:(t + 1) * P], xl[:, b, t], ident)
                last.then_inc(xlT_psum, 1)

            def queries(b):
                pe.wait_ge(xlT_made, b + 1)
                if b:
                    pe.wait_ge(q_made, b)
                nc.tensor.matmul(QW[:], par("wqT"), xlT[:, b], start=True, stop=True).then_inc(q_psum, 1)

            def scores(n):
                b, t = n // T, n % T
                if t == 0:
                    pe.wait_ge(q_made, b + 1)
                    pe.wait_ge(kbd_made, b + 1)
                if b:
                    pe.wait_ge(sd_made, n - T + 1)
                nc.tensor.matmul(SC[t][:], qT[:, b, t * P:(t + 1) * P], KBD[:, b].rearrange("p h k -> p (h k)"),
                                 start=True, stop=True).then_inc(scores_psum, 1)

            def transpose_probs(n):
                pe.wait_ge(pr_made, n + 1)
                if n >= 2:
                    pe.wait_ge(on_made, n - 1)
                for g in range(G):
                    last = nc.tensor.transpose(PT[n % 2][:, g * P:(g + 1) * P],
                                               pr[:, n // T, n % T, g * P:(g + 1) * P], ident)
                last.then_inc(pT_psum, 1)

            def values(n):
                pe.wait_ge(pT_made, n + 1)
                for g in range(G):
                    last = nc.tensor.matmul(PT[n % 2][:, g * HG * VW:(g + 1) * HG * VW],
                                            pT[:, n // T, n % T, g * P:(g + 1) * P],
                                            VBD[:, n // T, g].rearrange("p j d -> p (j d)"), start=True, stop=True)
                last.then_inc(pv_psum, 1)

            def transpose_output(b):
                for t in range(T):
                    pe.wait_ge(on_made, b * T + t + 1)
                    last = nc.tensor.transpose(XT[:, t * P:(t + 1) * P], on[:, b, t], ident)
                last.then_inc(oT_psum, 1)

            def combine(b):
                pe.wait_ge(oT_made, b + 1)
                if b:
                    pe.wait_ge(x1_made, b)
                for t in range(T):
                    last = nc.tensor.matmul(QW[:, t * P:(t + 1) * P], oT[:, b, t * P:(t + 1) * P], par("woT"),
                                            start=True, stop=True)
                last.then_inc(wo_psum, 1)

            def transpose_xn(b):
                for t in range(T):
                    pe.wait_ge(xn_made, b * T + t + 1)
                    last = nc.tensor.transpose(XNT[b][:, t * P:(t + 1) * P], xn[:, b, t], ident)
                last.then_inc(xnT_psum, 1)

            def transpose_base(b):
                pe.wait_ge(base_made, T * (b + 1))
                if b == 0:
                    pe.wait_ge(gT_made, 2)
                for t in range(T):
                    last = nc.tensor.transpose(BST[b][:, t * P:(t + 1) * P], base[:, b, t], ident)
                last.then_inc(baseT_psum, 1)

            def logits(b):
                pe.wait_ge(xh_made, b + 1)
                pe.wait_ge(xlo_made, b + 1)
                pe.wait_ge(wgl_made, 1)
                if b:
                    pe.wait_ge(gT_made, 1)
                for t in range(T):
                    o, c = LGP[b][:, t * E:(t + 1) * E], slice(t * P, (t + 1) * P)
                    nc.tensor.matmul(o, xh[:, b, c], wgh[:], start=True, stop=False)
                    nc.tensor.matmul(o, xlo[:, b, c], wgh[:], start=False, stop=False)
                    last = nc.tensor.matmul(o, xh[:, b, c], wgl[:], start=False, stop=True)
                last.then_inc(lg_psum, 1)

            def transpose_gates(b):
                pe.wait_ge(gate_made, b + 1)
                if b:
                    pe.wait_ge(lg_made, 2)
                for t in range(T):
                    last = nc.tensor.transpose(GTP[b][0:E, t * P:(t + 1) * P], gate[:, b, t], ident)
                last.then_inc(gT_psum, 1)

            def bias_term(b):
                pe.wait_ge(gT_made, b + 1)
                pe.wait_ge(b2_in, 16)
                pe.wait_ge(x1_made, 2)
                nc.tensor.matmul(ACC[b][:], b2_sb[:], gT[:, b], start=True, stop=False, skip_group_check=True)

            def up(n, j):
                s, b = j % Q, j // Q
                if isinstance(n, int) and n < Q:
                    pe.wait_ge(first_w1l, n + 1)
                    pe.wait_ge(lg_made, 1)
                for cols, dst, done, read in ((slice(I, 2 * I), HB[j % 2], hb_psum, bt_made),
                                              (slice(0, I), HA[j % 2], ha_psum, ge_made)):
                    if not isinstance(n, int) or n >= 2:
                        pe.wait_ge(read, n - 1)
                    nc.tensor.matmul(dst[:], w1h[s][:, cols], xh[:, b], start=True, stop=False)
                    nc.tensor.matmul(dst[:], w1h[s][:, cols], xlo[:, b], start=False, stop=False)
                    nc.tensor.matmul(dst[:], w1l[s][:, cols], xh[:, b], start=False, stop=True).then_inc(done, 1)

            def down(n, j, q, last=False):
                s, b = j % Q, j // Q
                pe.wait_ge(sg_made, n + 1)
                if b == 0:
                    pe.wait_ge(w2_in[s], q * 16 + 16)
                nc.tensor.matmul(ACC[b][:], w2s[s][:], sg[j % NS][:], start=False, stop=last,
                                 skip_group_check=True).then_inc(down_done, 1)

            pe.wait_ge(warm_set, 1)
            warm_up(5)
            pe.wait_ge(ctx_in, 16)
            pe.wait_ge(ctx4_made, 1)
            nc.tensor.matmul(PT[0][:, 0:B * KV], cpar("wkT"), cpar("ctxT"), start=True, stop=True).then_inc(kv_psum, 1)
            for b in range(B):
                last = nc.tensor.matmul(PT[1][:, b * D:(b + 1) * D], ctx4[:, b].rearrange("c g k -> c (g k)"),
                                        cpar("wvT"), start=True, stop=True)
            last.then_inc(kv_psum, 1)
            pe.wait_ge(pk_in, 16)
            project(0)
            queries(0)
            project(1)
            pe.wait_ge(vbd_made, (G + 1) * B)
            for n in range(B * T + 3):
                if n == 2:
                    queries(1)
                if n < B * T:
                    scores(n)
                if n >= 3:
                    values(n - 3)
                if 2 <= n < B * T + 2:
                    transpose_probs(n - 2)
                if n == T + LAG:
                    transpose_output(0)
                if n == T + LAG + 1:
                    combine(0)
            transpose_output(1)
            transpose_xn(0)
            combine(1)
            logits(0)

            up(0, 0)
            transpose_xn(1)
            transpose_gates(0)
            up(1, 1)
            logits(1)
            bias_term(0)
            down(0, 0, 0)
            up(2, 2)
            transpose_gates(1)
            down(1, 1, 0)
            up(3, 3)
            transpose_base(1)
            bias_term(1)
            transpose_base(0)

            def step(q, k):
                n, j = q * (B * Q) + (Q + k), (Q + k) % (B * Q)
                if k >= Q:
                    pe.wait_ge(w1l_made, q * Q + (k - Q + 1))
                up(n, j)
                down(n - 2, (j - 2) % (B * Q), q + (1 if k - 2 >= Q else 0))

            with pe.Fori(0, QUADS - 1) as q:
                for k in range(B * Q):
                    step(q, k)
            for k in range(Q):
                step(QUADS - 1, k)
            for n in (B * E - 2, B * E - 1):
                down(n, n % (B * Q), QUADS - 1, last=True)


def kernel(x, ctx_768, L0_xattn_Wq, L0_xattn_bq, L0_xattn_Wk, L0_xattn_bk, L0_xattn_Wv, L0_xattn_bv,
           L0_xattn_Wo, L0_xattn_bo, L0_ffn_norm_scale, L0_ffn_wg, L0_ffn_bg, L0_ffn_w1, L0_ffn_b1,
           L0_ffn_w2, L0_ffn_b2):
    import numpy as np
    import concourse.bacc as bacc
    from concourse.bass_utils import run_bass_kernel_spmd

    a = [np.asarray(v) for v in (x, ctx_768, L0_xattn_Wq, L0_xattn_bq, L0_xattn_Wk, L0_xattn_bk, L0_xattn_Wv,
                                 L0_xattn_bv, L0_xattn_Wo, L0_xattn_bo, L0_ffn_norm_scale, L0_ffn_wg, L0_ffn_bg,
                                 L0_ffn_w1, L0_ffn_b1, L0_ffn_w2, L0_ffn_b2)]
    x, ctx, wq, bq, wk, bk, wv, bv, wo, bo, ns, wg, bg, w1, b1, w2, b2 = a
    f = np.float32
    p = np.arange(P)
    ident = np.eye(P, dtype=f)
    head_mask = (p[:, None] // HD == np.arange(H)[None]).astype(f)
    group_mask = (p[:, None] // KV == np.arange(HG)[None]).astype(f)
    iota = np.broadcast_to(np.arange(E, dtype=f), (P, E))
    pack = np.concatenate([wq.T, wo.T, ident, wg, head_mask, group_mask, iota, bq[:, None], ns[:, None]], axis=1)
    ctx_pack = np.concatenate([
        np.concatenate([wk.T, bk[None]], axis=0),
        np.concatenate([wv.T, bv[None]], axis=0),
        np.concatenate([ctx.reshape(B * KV, C).T, np.ones((1, B * KV), f)], axis=0)], axis=1)
    w1s = w1.reshape(E, D, I, 2).transpose(1, 0, 3, 2).reshape(D, E * W1)
    b1s = b1.reshape(E, I, 2).transpose(1, 2, 0).reshape(I, 2 * E)
    rows = np.concatenate([bo, bg])
    arrays = {"x": x, "pack": pack, "ctx": ctx_pack, "rows": rows, "b2": b2, "w1": w1s, "w2": w2,
              "b1": b1s}
    arrays = {k: np.ascontiguousarray(v) for k, v in arrays.items()}
    nc = bacc.Bacc("TRN2", target_bir_lowering=False, num_devices=1)
    args = [nc.dram_tensor(f"in_{k}", v.shape, mybir.dt.from_np(v.dtype), kind="ExternalInput").ap()
            for k, v in arrays.items()]
    out = nc.dram_tensor("out", (D, B, N), FP32, kind="ExternalOutput").ap()
    build(nc, *args, out)
    r = run_bass_kernel_spmd(nc, [{f"in_{k}": v for k, v in arrays.items()}], core_ids=[0])
    got = r.results[0]["out"]
    return np.ascontiguousarray(got.reshape(D, B, T, P).transpose(1, 3, 2, 0).reshape(B, N, D))
```

```python
import concourse.bass as bass
from concourse import mybir
from contextlib import ExitStack

FP32 = mybir.dt.float32
FP32R = mybir.dt.float32r
BF16 = mybir.dt.bfloat16
U32 = mybir.dt.uint32
ALU = mybir.AluOpType
ACT = mybir.ActivationFunctionType
AX = mybir.AxisListType

B = 2
T = 4
P = 128
N = T * P
D = 128
C = 96
KV = 32
H = 16
HD = D // H
G = 4
HG = H // G
VW = HD + 1
E = 16
I = 128
K = 4
WARM = (9, 1)
TOP = 8
SCALE = 1.0 / float(HD) ** 0.5
EPS = 1e-5
LIMIT = 7.0
ALPHA = 1.702
GELU_AT_LIMIT = LIMIT / (1.0 + 2.718281828459045 ** (-ALPHA * LIMIT))

PACK = {}
_at = 0
for _name, _n in (("wqT", D), ("woT", D), ("ident", P), ("wg", E), ("head_mask", H), ("group_mask", HG),
                  ("iota", E), ("bq", 1), ("norm_scale", 1)):
    PACK[_name] = (_at, _at + _n)
    _at += _n
PACK_COLS = _at
CTX = {"wkT": (0, D), "wvT": (D, 2 * D), "ctxT": (2 * D, 2 * D + B * KV)}
CTX_COLS = 2 * D + B * KV
W1 = 2 * I
NORM_STEPS = ((0, 0, T // 2), (0, T // 2, T), (1, 0, T))
HALVES = (slice(0, N // 2), slice(N // 2, N))
Q = 4
QUADS = E // Q


def build(nc, x, pack, ctx, rows, b2, w1, w2, b1, out):
    gate_rows = nc.dram_tensor("gate_rows", (E, B, N), FP32).ap()
    st = ExitStack()
    with st:
        def sb(name, shape, dt=FP32):
            return st.enter_context(nc.sbuf_tensor(name, shape, dt))

        def sem(name):
            return st.enter_context(nc.semaphore(name))

        x_sb = sb("x_sb", [P, B, T, D])
        pk = sb("pk", [P, PACK_COLS])
        cx = sb("cx", [C + 1, CTX_COLS])
        row_sb = sb("row_sb", [P, D + E])
        b2_sb = sb("b2_sb", [E, D])
        w1_sb = sb("w1_sb", [D, E * W1])
        b1_sb = sb("b1_sb", [I, 2 * E])
        b1p = sb("b1p", [I, E])

        def par(name):
            return pk[:, PACK[name][0]:PACK[name][1]]

        def cpar(name):
            return cx[:, CTX[name][0]:CTX[name][1]]
        ident = par("ident")
        half = sb("half", [P, T])
        ctx4 = sb("ctx4", [C + 1, B, G, KV])
        KBD = sb("KBD", [D, B, H, KV])
        VBD = sb("VBD", [P, B, G, HG, VW])
        xb = sb("xb", [P, B, T, D])
        stats = sb("stats", [P, B, T, 6])
        mv = sb("mv", [P, B, T, 2])
        ve = sb("ve", [P, B, T])
        rstd = sb("rstd", [P, B, T])
        xl = sb("xl", [P, B, T, D])
        xlT = sb("xlT", [D, B, N])
        qT = sb("qT", [D, B, N])
        mx = sb("mx", [P, B, T, H])
        sd = sb("sd", [P, B, T, H * KV])
        pr = sb("pr", [P, B, T, H * KV])
        pT = sb("pT", [P, B, T, G * P])
        rs = sb("rs", [P, B, T, H])
        on = sb("on", [P, B, T, D])
        oT = sb("oT", [D, B, N])
        x1 = sb("x1", [P, B, T, D])
        stats2 = sb("stats2", [P, B, T, 6])
        mv2 = sb("mv2", [P, B, T, 2])
        v2a = sb("v2a", [P, B, T])
        v2b = sb("v2b", [P, B, T])
        r12 = sb("r12", [P, B, T])
        r1 = sb("r1", [P, B, T])
        mr12 = sb("mr12", [P, T])
        nmr12 = sb("nmr12", [P, T])
        r1p = sb("r1p", [P, B, T])
        mr = sb("mr", [P, B, T])
        nmr = sb("nmr", [P, B, T])
        xn = sb("xn", [P, B, T, D])
        base = sb("base", [P, B, T, D])
        baseT = sb("baseT", [D, B, N])
        xh = sb("xh", [D, B, N], FP32R)
        xlo = sb("xlo", [D, B, N], FP32R)
        wgs = sb("wgs", [D, 2 * E], FP32R)
        lgb = sb("lgb", [P, B, T, E])
        lg = sb("lg", [P, B, T, E])
        top = sb("top", [P, B, T, TOP])
        idx = sb("idx", [P, B, T, TOP], U32)
        idf = sb("idf", [P, B, T, K])
        td = sb("td", [P, B, T, K])
        te = sb("te", [P, B, T, K])
        ts = sb("ts", [P, B, T])
        tr = sb("tr", [P, B, T])
        gk = sb("gk", [P, B, T, K])
        oh = sb("oh", [P, B, T * K, E])
        og = sb("og", [P, B, T * K, E])
        gate = sb("gate", [P, B, T, E])
        gT = sb("gT", [E, B, N])
        w1h = [sb(f"w1h{s}", [D, W1], FP32R) for s in range(Q)]
        w1l = [sb(f"w1l{s}", [D, W1], FP32R) for s in range(Q)]
        w2s = [sb(f"w2s{s}", [I, D]) for s in range(Q)]
        gates_sb = [[sb(f"gates{b}{s}", [P, N]) for s in range(Q)] for b in range(B)]
        NS = 4
        ge = [sb(f"ge{s}", [I, N]) for s in range(NS)]
        bt = [sb(f"bt{s}", [I, N]) for s in range(NS)]
        pg = [sb(f"pg{s}", [I, N]) for s in range(NS)]
        sg = [sb(f"sg{s}", [I, N]) for s in range(NS)]
        sum0 = sb("sum0", [D, N])
        o_most = sb("o_most", [D, N])
        o_sb = sb("o_sb", [D, B, N])
        warm = sb("warm", [P, N], BF16)

        bank = [st.enter_context(nc.psum_tensor(f"bank{i}", [P, N], FP32)) for i in range(8)]
        XT, QW = bank[0], bank[1]
        SC = bank[2:6]
        PT = bank[6:8]
        XNT = [bank[2], bank[7]]
        LGP = [bank[3], bank[7]]
        GTP = [bank[0], bank[1]]
        BST = bank[6]
        GB = [bank[6], bank[1], bank[6], bank[7]]
        ACC = bank[0:2]
        QUERY_STEPS = ((0, slice(0, N // 2), bank[0], bank[1]), (0, slice(N // 2, N), bank[4], bank[5]),
                       (1, slice(0, N), bank[0], bank[1]))
        HB = bank[2:4]
        LAST = bank[2:4]
        HA = bank[4:6]

        pk_in = sem("pk_in")
        x_in = [sem(f"x_in{b}") for b in range(B)]
        ctx_in = sem("ctx_in")
        rows_in = sem("rows_in")
        b1_in = sem("b1_in")
        b2_in = sem("b2_in")
        w1_in = [sem(f"w1_in{q}") for q in range(QUADS)]
        w2_in = [sem(f"w2_in{s}") for s in range(Q)]
        gates_in = [[sem(f"gates_in{b}{s}") for s in range(Q)] for b in range(B)]
        half_set = sem("half_set"); warm_set = sem("warm_set")
        ctx4_made = sem("ctx4_made"); kv_psum = sem("kv_psum");
        kbd_made = sem("kbd_made"); vbd_made = sem("vbd_made"); xb_made = sem("xb_made")
        stats_made = sem("stats_made"); mv_made = sem("mv_made"); ve_made = sem("ve_made")
        rstd_made = sem("rstd_made"); xl_made = sem("xl_made"); xlT_psum = sem("xlT_psum")
        xlT_made = sem("xlT_made"); q_psum = sem("q_psum"); q_made = sem("q_made")
        scores_psum = sem("scores_psum"); mx_made = sem("mx_made"); sd_made = sem("sd_made")
        pr_made = sem("pr_made"); pT_psum = sem("pT_psum"); pT_made = sem("pT_made"); pv_psum = sem("pv_psum")
        rs_made = sem("rs_made"); on_made = sem("on_made"); oT_psum = sem("oT_psum"); oT_made = sem("oT_made")
        wo_psum = sem("wo_psum"); x1_made = sem("x1_made"); stats2_made = sem("stats2_made")
        mv2_made = sem("mv2_made"); v2a_made = sem("v2a_made"); v2b_made = sem("v2b_made")
        r12_made = sem("r12_made"); r1_made = sem("r1_made"); mr_made = sem("mr_made"); nmr_made = sem("nmr_made")
        mr12_made = sem("mr12_made"); nmr12_made = sem("nmr12_made")
        xn_made = sem("xn_made"); base_made = sem("base_made"); xnT_psum = sem("xnT_psum")
        baseT_psum = sem("baseT_psum"); baseT_made = sem("baseT_made")
        wgh_made = sem("wgh_made"); wgl_made = sem("wgl_made"); xh_made = sem("xh_made"); xlo_made = sem("xlo_made")
        lg_psum = sem("lg_psum"); lgb_made = sem("lgb_made"); lg_made = sem("lg_made")
        top_made = sem("top_made"); idx_made = sem("idx_made")
        idf_made = sem("idf_made"); td_made = sem("td_made"); te_made = sem("te_made"); ts_made = sem("ts_made")
        tr_made = sem("tr_made"); gk_made = sem("gk_made"); oh_made = sem("oh_made"); og_made = sem("og_made")
        gate_made = sem("gate_made"); gT_psum = sem("gT_psum"); gT_made = sem("gT_made")
        gates_out = [sem(f"gates_out{b}") for b in range(B)]
        b1p_made = sem("b1p_made")
        gb_psum = sem("gb_psum")
        first_w1h = sem("first_w1h"); first_w1l = sem("first_w1l")
        w1h_made = sem("w1h_made"); w1l_made = sem("w1l_made")
        hb_psum = sem("hb_psum"); ha_psum = sem("ha_psum")
        ge_made = sem("ge_made"); bt_made = sem("bt_made"); pg_made = sem("pg_made"); sg_made = sem("sg_made")
        down_done = sem("down_done"); sum0_made = sem("sum0_made")
        o_most_made = sem("o_most_made"); o_made = sem("o_made"); o0_made = sem("o0_made")
        out_done = [sem(f"out_done{i}") for i in range(3)]

        def raw_w1(e):
            return w1_sb[:, bass.ds(e * W1, W1)]

        block = st.enter_context(nc.Block())

        @block.sync
        def _(sp):
            sp.dma_start(x_sb[:, 0], x[0].rearrange("(p t) c -> p t c", t=T)).then_inc(x_in[0], 16)
            sp.dma_start(x_sb[:, 1], x[1].rearrange("(p t) c -> p t c", t=T)).then_inc(x_in[1], 16)
            sp.dma_start(row_sb[:, 0:D], rows[0:D].partition_broadcast(P)).then_inc(rows_in, 16)
            sp.dma_start(row_sb[:, D:D + E], rows[D:D + E].partition_broadcast(P)).then_inc(rows_in, 16)
            for q in range(QUADS):
                sp.dma_start(w1_sb[:, q * Q * W1:(q + 1) * Q * W1],
                             w1[:, q * Q * W1:(q + 1) * Q * W1]).then_inc(w1_in[q], 16)
                if q == 0:
                    for s in range(Q):
                        sp.dma_start(w2s[s][:], w2[s]).then_inc(w2_in[s], 16)
                    sp.dma_start(b1_sb[:], b1).then_inc(b1_in, 16)
                    sp.dma_start(b2_sb[:], b2).then_inc(b2_in, 16)
            for b in range(B):
                sp.wait_ge(gT_made, b + 1)
                sp.dma_start(gate_rows[:, b], gT[:, b]).then_inc(gates_out[b], 16)
                sp.wait_ge(gates_out[b], 16)
                for s in range(2, Q):
                    sp.dma_start(gates_sb[b][s][:], gate_rows[s, b].partition_broadcast(P)
                                 ).then_inc(gates_in[b][s], 16)
            with sp.Fori(0, QUADS - 1) as q:
                for b in range(B):
                    for s in range(Q):
                        sp.wait_ge(pg_made, q * (B * Q) + (b * Q + s + 1))
                        sp.dma_start(gates_sb[b][s][:],
                                     gate_rows[bass.ds(q * Q + (Q + s), 1), b].partition_broadcast(P)
                                     ).then_inc(gates_in[b][s], 16)
                        if b == B - 1:
                            sp.wait_ge(down_done, q * (B * Q) + (b * Q + s + 1))
                            sp.dma_start(w2s[s][:], w2[bass.ds(q * Q + (Q + s), 1)].rearrange("a i d -> (a i) d")
                                         ).then_inc(w2_in[s], 16)
            sp.wait_ge(o0_made, 1)
            sp.dma_start(out[:, 0], o_sb[:, 0]).then_inc(out_done[0], 16)
            for i, cols in enumerate(HALVES):
                sp.wait_ge(o_made, i + 1)
                sp.dma_start(out[:, 1, cols], o_sb[:, 1, cols]).then_inc(out_done[1 + i], 16)
            for i in range(3):
                sp.wait_ge(out_done[i], 16)

        @block.gpsimd
        def _(pool):
            nc.gpsimd.memset(half[:], -0.5).then_inc(half_set, 1)
            pool.wait_ge(half_set, 1)
            for i, (b, lo, hi) in enumerate(NORM_STEPS):
                pool.wait_ge(ve_made, i + 1)
                nc.gpsimd.tensor_tensor(rstd[:, b, lo:hi], ve[:, b, lo:hi], half[:, 0:hi - lo],
                                        ALU.pow).then_inc(rstd_made, 1)
            pool.wait_ge(rows_in, 32)
            for b in range(B):
                pool.wait_ge(x_in[b], 16)
                nc.gpsimd.tensor_tensor(xb[:, b], x_sb[:, b],
                                        row_sb[:, 0:D].unsqueeze(1).to_broadcast([P, T, D]),
                                        ALU.add).then_inc(xb_made, 1)
            pool.wait_ge(pk_in, 16)
            nc.gpsimd.tensor_copy(wgs[:, 0:E], par("wg")).then_inc(wgh_made, 1)
            pool.wait_ge(wgh_made, 1)
            nc.gpsimd.tensor_tensor(wgs[:, E:2 * E], par("wg"), wgs[:, 0:E].bitcast(FP32),
                                    ALU.subtract).then_inc(wgl_made, 1)
            pool.wait_ge(w1_in[0], 16)
            for s in range(Q):
                nc.gpsimd.tensor_copy(w1h[s][:], raw_w1(s)).then_inc(first_w1h, 1)
                pool.wait_ge(first_w1h, s + 1)
                nc.gpsimd.tensor_tensor(w1l[s][:], raw_w1(s), w1h[s][:].bitcast(FP32),
                                        ALU.subtract).then_inc(first_w1l, 1)
            pool.wait_ge(b1_in, 16)
            nc.gpsimd.tensor_scalar(b1p[:], b1_sb[:, E:2 * E], 1.0, None, ALU.add).then_inc(b1p_made, 1)
            for b in range(B):
                pool.wait_ge(v2b_made, b + 1)
                nc.gpsimd.tensor_tensor(r12[:, b], v2b[:, b], half[:], ALU.pow).then_inc(r12_made, 1)
                if b:
                    pool.wait_ge(r12_made, b + 1)
                    nc.gpsimd.tensor_tensor(mr12[:], mv2[:, b, :, 0], r12[:, b], ALU.mult).then_inc(mr12_made, 1)
                    pool.wait_ge(mr12_made, 1)
                    nc.gpsimd.tensor_scalar(nmr12[:], mr12[:], -1.0, None, ALU.mult).then_inc(nmr12_made, 1)
                pool.wait_ge(v2a_made, b + 1)
                nc.gpsimd.tensor_tensor(r1[:, b], v2a[:, b], half[:], ALU.pow).then_inc(r1_made, 1)
                pool.wait_ge(r1_made, b + 1)
                nc.gpsimd.tensor_tensor(mr[:, b], mv2[:, b, :, 0], r1[:, b], ALU.mult).then_inc(mr_made, 1)
                nc.gpsimd.tensor_scalar(r1p[:, b], r1[:, b], 1.0, None, ALU.add).then_inc(nmr_made, 1)
                pool.wait_ge(mr_made, b + 1)
                nc.gpsimd.tensor_scalar(nmr[:, b], mr[:, b], -1.0, None, ALU.mult).then_inc(nmr_made, 1)

            pool.wait_ge(sum0_made, 1)
            pool.wait_ge(baseT_made, B)
            nc.gpsimd.tensor_tensor(o_sb[:, 0], sum0[:], baseT[:, 0], ALU.add).then_inc(o0_made, 1)

        @block.vector
        def _(dve):
            def moments(i):
                b, lo, hi = NORM_STEPS[i]
                dve.wait_ge(x_in[b], 16)
                for t in range(lo, hi):
                    nc.vector.bn_stats(stats[:, b, t], x_sb[:, b, t]).then_inc(stats_made, 1)
                for t in range(lo, hi):
                    dve.wait_ge(stats_made, b * T + t + 1)
                    nc.vector.bn_aggr(mv[:, b, t], stats[:, b, t]).then_inc(mv_made, 1)
                dve.wait_ge(mv_made, b * T + hi)
                nc.vector.tensor_scalar(ve[:, b, lo:hi], mv[:, b, lo:hi, 1], EPS, None, ALU.add).then_inc(ve_made, 1)

            def normalise(i):
                b, lo, hi = NORM_STEPS[i]
                dve.wait_ge(rstd_made, i + 1)
                for t in range(lo, hi):
                    nc.vector.tensor_scalar(xl[:, b, t], x_sb[:, b, t], mv[:, b, t, 0:1], rstd[:, b, t:t + 1],
                                            ALU.subtract, ALU.mult).then_inc(xl_made, 1)

            def keys(b):
                dve.wait_ge(kv_psum, 1)
                dve.wait_ge(pk_in, 16)
                nc.vector.tensor_tensor(KBD[:, b], PT[0][:, b * KV:(b + 1) * KV].unsqueeze(1)
                                        .to_broadcast([D, H, KV]),
                                        par("head_mask").unsqueeze(2).to_broadcast([D, H, KV]),
                                        ALU.mult).then_inc(kbd_made, 1)

            def value_blocks():
                dve.wait_ge(kv_psum, 2)
                nc.vector.tensor_tensor(VBD[:, :, :, :, 0:HD].rearrange("p b g j d -> p (b g) j d"),
                                        PT[1][:, 0:B * D].rearrange("p (a j d) -> p a j d", j=HG, d=HD),
                                        par("group_mask").unsqueeze(1).unsqueeze(3)
                                        .to_broadcast([P, B * G, HG, HD]), ALU.mult).then_inc(vbd_made, 1)
                nc.vector.tensor_copy(VBD[:, :, :, :, HD].rearrange("p b g j -> p (b g) j"),
                                      par("group_mask").unsqueeze(1).to_broadcast([P, B * G, HG])
                                      ).then_inc(vbd_made, 1)

            def maximum(n):
                dve.wait_ge(scores_psum, n + 1)
                nc.vector.tensor_reduce(mx[:, n // T, n % T], SC[n % T][:].rearrange("p (h k) -> p h k", h=H),
                                        AX.X, ALU.max).then_inc(mx_made, 1)

            def less_maximum(n):
                dve.wait_ge(mx_made, n + 1)
                nc.vector.tensor_tensor(sd[:, n // T, n % T].rearrange("p (h k) -> p h k", h=H),
                                        SC[n % T][:].rearrange("p (h k) -> p h k", h=H),
                                        mx[:, n // T, n % T].unsqueeze(2).to_broadcast([P, H, KV]),
                                        ALU.subtract).then_inc(sd_made, 1)

            def divide(n):
                dve.wait_ge(pv_psum, n + 1)
                pv = PT[n % 2][:, 0:H * VW].rearrange("p (h d) -> p h d", h=H)
                nc.vector.reciprocal(rs[:, n // T, n % T], pv[:, :, HD]).then_inc(rs_made, 1)
                dve.wait_ge(rs_made, n + 1)
                nc.vector.tensor_tensor(on[:, n // T, n % T].rearrange("p (h d) -> p h d", h=H), pv[:, :, 0:HD],
                                        rs[:, n // T, n % T].unsqueeze(2).to_broadcast([P, H, HD]),
                                        ALU.mult).then_inc(on_made, 1)

            def residual(b):
                dve.wait_ge(wo_psum, b + 1)
                dve.wait_ge(xb_made, b + 1)
                nc.vector.tensor_tensor(x1[:, b], QW[:].rearrange("p (t c) -> p t c", t=T), xb[:, b],
                                        ALU.add).then_inc(x1_made, 1)
                dve.wait_ge(x1_made, b + 1)
                for t in range(T):
                    nc.vector.bn_stats(stats2[:, b, t], x1[:, b, t]).then_inc(stats2_made, 1)
                for t in range(T):
                    dve.wait_ge(stats2_made, b * T + t + 1)
                    nc.vector.bn_aggr(mv2[:, b, t], stats2[:, b, t]).then_inc(mv2_made, 1)
                dve.wait_ge(mv2_made, T * (b + 1))
                nc.vector.tensor_scalar(v2b[:, b], mv2[:, b, :, 1], 1.0 + EPS, EPS * EPS, ALU.mult,
                                        ALU.add).then_inc(v2b_made, 1)
                nc.vector.tensor_scalar(v2a[:, b], mv2[:, b, :, 1], EPS, None, ALU.add).then_inc(v2a_made, 1)

            def renormalise(b):
                dve.wait_ge(r12_made, b + 1)
                for t in range(T):
                    nc.vector.tensor_scalar(xn[:, b, t], x1[:, b, t], mv2[:, b, t, 0:1], r12[:, b, t:t + 1],
                                            ALU.subtract, ALU.mult).then_inc(xn_made, 1)

            def low_part(b):
                dve.wait_ge(xh_made, b + 1)
                nc.vector.scalar_tensor_tensor(xlo[:, b], XNT[b][:], par("norm_scale"), xh[:, b].bitcast(FP32),
                                               ALU.mult, ALU.subtract).then_inc(xlo_made, 1)

            def choose(b):
                dve.wait_ge(lg_psum, b + 1)
                parts = LGP[b][:, 0:2 * T * E].rearrange("p (t h e) -> p t h e", t=T, h=2)
                nc.vector.tensor_tensor(lgb[:, b], parts[:, :, 1], row_sb[:, D:D + E].unsqueeze(1)
                                        .to_broadcast([P, T, E]), ALU.add).then_inc(lgb_made, 1)
                dve.wait_ge(lgb_made, b + 1)
                nc.vector.tensor_tensor(lg[:, b], parts[:, :, 0], lgb[:, b], ALU.add).then_inc(lg_made, 1)
                dve.wait_ge(lg_made, b + 1)
                for t in range(T):
                    nc.vector.max(top[:, b, t], lg[:, b, t]).then_inc(top_made, 1)
                dve.wait_ge(top_made, T * (b + 1))
                nc.vector.tensor_tensor(td[:, b], top[:, b, :, 0:K], top[:, b, :, 0:1].to_broadcast([P, T, K]),
                                        ALU.subtract).then_inc(td_made, 1)
                for t in range(T):
                    nc.vector.max_index(idx[:, b, t], top[:, b, t], lg[:, b, t]).then_inc(idx_made, 1)
                dve.wait_ge(idx_made, T * (b + 1))
                nc.vector.tensor_copy(idf[:, b], idx[:, b, :, 0:K]).then_inc(idf_made, 1)

            def weigh(b):
                dve.wait_ge(te_made, b + 1)
                nc.vector.tensor_reduce(ts[:, b], te[:, b], AX.X, ALU.add).then_inc(ts_made, 1)
                dve.wait_ge(idf_made, b + 1)
                nc.vector.tensor_tensor(oh[:, b], par("iota").unsqueeze(1).to_broadcast([P, T * K, E]),
                                        idf[:, b].rearrange("p t k -> p (t k)").unsqueeze(2)
                                        .to_broadcast([P, T * K, E]), ALU.is_equal).then_inc(oh_made, 1)
                dve.wait_ge(ts_made, b + 1)
                nc.vector.reciprocal(tr[:, b], ts[:, b]).then_inc(tr_made, 1)
                dve.wait_ge(tr_made, b + 1)
                nc.vector.tensor_tensor(gk[:, b], te[:, b], tr[:, b].unsqueeze(2).to_broadcast([P, T, K]),
                                        ALU.mult).then_inc(gk_made, 1)
                dve.wait_ge(gk_made, b + 1)
                dve.wait_ge(oh_made, b + 1)
                nc.vector.tensor_tensor(og[:, b], oh[:, b],
                                        gk[:, b].rearrange("p t k -> p (t k)").unsqueeze(2)
                                        .to_broadcast([P, T * K, E]), ALU.mult).then_inc(og_made, 1)
                dve.wait_ge(og_made, b + 1)
                nc.vector.tensor_reduce(gate[:, b], og[:, b].rearrange("p (t k) e -> p t e k", t=T),
                                        AX.X, ALU.add).then_inc(gate_made, 1)

            def upper(n, j, e):
                dve.wait_ge(hb_psum, n + 1)
                nc.vector.tensor_scalar(bt[j % NS][:], HB[j % 2][:], b1p[:, bass.ds(e, 1)], LIMIT + 1.0,
                                        ALU.add, ALU.min).then_inc(bt_made, 1)

            def gated(n, j, q):
                dve.wait_ge(bt_made, n + 1)
                dve.wait_ge(gates_in[j // Q][j % Q], q * 16 + (0 if j < 2 else 16))
                nc.vector.scalar_tensor_tensor(pg[j % NS][:], bt[j % NS][:], 1.0 - LIMIT, gates_sb[j // Q][j % Q][:],
                                               ALU.max, ALU.mult).then_inc(pg_made, 1)

            def first_gated(n):
                dve.wait_ge(bt_made, n + 1)
                dve.wait_ge(gb_psum, n + 1)
                nc.vector.scalar_tensor_tensor(pg[n][:], bt[n][:], 1.0 - LIMIT, GB[n][:],
                                               ALU.max, ALU.mult).then_inc(pg_made, 1)

            def product(n, j):
                dve.wait_ge(ge_made, n + 1)
                dve.wait_ge(pg_made, n + 1)
                nc.vector.scalar_tensor_tensor(sg[j % NS][:], ge[j % NS][:], GELU_AT_LIMIT, pg[j % NS][:],
                                               ALU.min, ALU.mult).then_inc(sg_made, 1)

            nc.vector.memset(warm[:], 0.0).then_inc(warm_set, 1)
            moments(0)
            moments(1)
            normalise(0)
            normalise(1)
            keys(0)
            moments(2)
            value_blocks()
            keys(1)
            maximum(0)
            normalise(2)
            maximum(1)
            less_maximum(0)
            less_maximum(1)
            maximum(2)
            maximum(3)
            less_maximum(2)
            less_maximum(3)
            maximum(4)
            less_maximum(4)
            divide(0)
            divide(1)
            maximum(5)
            less_maximum(5)
            maximum(6)
            less_maximum(6)
            divide(2)
            divide(3)
            maximum(7)
            divide(4)
            less_maximum(7)
            divide(5)
            residual(0)
            divide(6)
            divide(7)
            renormalise(0)
            low_part(0)
            residual(1)
            dve.wait_ge(rows_in, 32)
            choose(0)
            dve.wait_ge(b1p_made, 1)
            upper(0, 0, 0)
            weigh(0)
            upper(1, 1, 1)
            upper(2, 2, 2)
            first_gated(0)
            product(0, 0)
            low_part(1)
            first_gated(1)
            product(1, 1)
            choose(1)
            weigh(1)
            gated(2, 2, 0)
            product(2, 2)
            upper(3, 3, 3)
            gated(3, 3, 0)

            def step(q, k):
                n, j = q * (B * Q) + (Q + k), (Q + k) % (B * Q)
                later = k // Q
                upper(n, j, q * Q + (Q * later + j % Q))
                product(n - 1, (j - 1) % (B * Q))
                gated(n, j, q + later)

            with dve.Fori(0, QUADS - 1) as q:
                for k in range(B * Q):
                    step(q, k)
                    if 1 <= k <= Q:
                        s = k - 1
                        dve.wait_ge(w1h_made, q * Q + (s + 1))
                        nc.vector.tensor_tensor(w1l[s][:], raw_w1(q * Q + (Q + s)), w1h[s][:].bitcast(FP32),
                                                ALU.subtract).then_inc(w1l_made, 1)
            for k in range(Q):
                step(QUADS - 1, k)
            dve.wait_ge(ge_made, B * E)
            dve.wait_ge(pg_made, B * E)
            for cols in HALVES:
                nc.vector.scalar_tensor_tensor(sg[NS - 1][:, cols], ge[NS - 1][:, cols], GELU_AT_LIMIT,
                                               pg[NS - 1][:, cols], ALU.min, ALU.mult).then_inc(sg_made, 1)
            dve.wait_ge(down_done, B * E - 1)
            dve.wait_ge(baseT_made, B)
            nc.vector.tensor_tensor(o_most[:], ACC[1][:], baseT[:, 1], ALU.add).then_inc(o_most_made, 1)
            dve.wait_ge(o_most_made, 1)
            for i, cols in enumerate(HALVES):
                dve.wait_ge(down_done, B * E + i)
                nc.vector.tensor_tensor(o_sb[:, 1, cols], LAST[i][:, cols], o_most[:, cols],
                                        ALU.add).then_inc(o_made, 1)

        @block.scalar
        def _(act):
            act.dma_start(cx[:], ctx).then_inc(ctx_in, 16)
            act.dma_start(pk[:], pack).then_inc(pk_in, 16)
            nc.scalar.preload_act_table(ACT.Exp)
            act.wait_ge(ctx_in, 16)
            nc.scalar.copy(ctx4[:], cpar("ctxT").rearrange("c (b k) -> c b k", b=B).unsqueeze(2)
                           .to_broadcast([C + 1, B, G, KV])).then_inc(ctx4_made, 1)

            def project_out(i):
                b, cols, xt, _ = QUERY_STEPS[i]
                act.wait_ge(xlT_psum, i + 1)
                nc.scalar.copy(xlT[:, b, cols], xt[:, cols]).then_inc(xlT_made, 1)

            def query(i):
                b, cols, _, qw = QUERY_STEPS[i]
                act.wait_ge(q_psum, i + 1)
                nc.scalar.activation(qT[:, b, cols], qw[:, cols], ACT.Identity, bias=par("bq")).then_inc(q_made, 1)

            def exponential(n):
                act.wait_ge(sd_made, n + 1)
                nc.scalar.activation(pr[:, n // T, n % T], sd[:, n // T, n % T], ACT.Exp,
                                     scale=SCALE).then_inc(pr_made, 1)

            def out_of_psum(n):
                act.wait_ge(pT_psum, n + 1)
                nc.scalar.copy(pT[:, n // T, n % T], PT[n % 2][:]).then_inc(pT_made, 1)

            def output(b):
                act.wait_ge(oT_psum, b + 1)
                nc.scalar.copy(oT[:, b], XT[:]).then_inc(oT_made, 1)

            def bases(b):
                act.wait_ge(nmr_made, 2 * (b + 1))
                for t in range(T):
                    nc.scalar.activation(base[:, b, t], x1[:, b, t], ACT.Identity, bias=nmr[:, b, t:t + 1],
                                         scale=r1p[:, b, t:t + 1]).then_inc(base_made, 1)

            def renormalise_1():
                act.wait_ge(nmr12_made, 1)
                for t in range(T):
                    nc.scalar.activation(xn[:, 1, t], x1[:, 1, t], ACT.Identity, bias=nmr12[:, t:t + 1],
                                         scale=r12[:, 1, t:t + 1]).then_inc(xn_made, 1)

            def spread_out(s):
                act.wait_ge(gb_psum, 3 + s)
                nc.scalar.copy(gates_sb[1][s][:], bank[6 + s][:]).then_inc(gates_in[1][s], 16)

            def high_part(b):
                act.wait_ge(xnT_psum, b + 1)
                nc.scalar.activation(xh[:, b], XNT[b][:], ACT.Copy, scale=par("norm_scale")).then_inc(xh_made, 1)

            def base_out(b):
                act.wait_ge(baseT_psum, b + 1)
                nc.scalar.copy(baseT[:, b], BST[:]).then_inc(baseT_made, 1)

            def choice(b):
                act.wait_ge(td_made, b + 1)
                nc.scalar.activation(te[:, b], td[:, b], ACT.Exp).then_inc(te_made, 1)

            def gates(b):
                act.wait_ge(gT_psum, b + 1)
                nc.scalar.copy(gT[:, b], GTP[b][0:E, :]).then_inc(gT_made, 1)

            def activate(n, j, e):
                act.wait_ge(ha_psum, n + 1)
                nc.scalar.activation(ge[j % NS][:], HA[j % 2][:], ACT.Gelu_apprx_sigmoid,
                                     bias=b1_sb[:, bass.ds(e, 1)]).then_inc(ge_made, 1)

            act.wait_ge(pk_in, 16)
            project_out(0)
            project_out(1)
            query(0)
            query(1)
            project_out(2)
            exponential(0)
            exponential(1)
            query(2)
            out_of_psum(0)
            out_of_psum(1)
            exponential(2)
            exponential(3)
            exponential(4)
            out_of_psum(2)
            out_of_psum(3)
            exponential(5)
            exponential(6)
            out_of_psum(4)
            out_of_psum(5)
            output(0)
            exponential(7)
            out_of_psum(6)
            out_of_psum(7)
            output(1)
            high_part(0)
            bases(0)
            choice(0)
            nc.scalar.preload_act_table(ACT.Gelu_apprx_sigmoid)
            base_out(0)
            renormalise_1()
            act.wait_ge(b1_in, 16)
            activate(0, 0, 0)
            activate(1, 1, 1)
            high_part(1)
            gates(0)
            activate(2, 2, 2)
            activate(3, 3, 3)
            nc.scalar.preload_act_table(ACT.Exp)
            choice(1)
            bases(1)
            nc.scalar.preload_act_table(ACT.Gelu_apprx_sigmoid)
            gates(1)
            spread_out(0)
            spread_out(1)
            base_out(1)

            def step(q, k):
                n, j = q * (B * Q) + (Q + k), (Q + k) % (B * Q)
                activate(n, j, q * Q + (Q * (k // Q) + j % Q))

            for q in range(1, QUADS):
                act.wait_ge(w1_in[q], 16)
            with act.Fori(0, QUADS - 1) as q:
                for k in range(B * Q):
                    step(q, k)
                    if k < Q:
                        nc.scalar.copy(w1h[k][:], raw_w1(q * Q + (Q + k))).then_inc(w1h_made, 1)
            for k in range(Q):
                step(QUADS - 1, k)
                if k == 1:
                    act.wait_ge(down_done, B * E - Q)
                    nc.scalar.copy(sum0[:], ACC[0][:]).then_inc(sum0_made, 1)

        @block.tensor
        def _(pe):
            def warm_up(count):
                for _ in range(count):
                    nc.tensor.matmul(bank[5][:], warm[:, 0:P], warm[:], start=True, stop=True)

            def project(i):
                b, cols, xt, _ = QUERY_STEPS[i]
                if b:
                    pe.wait_ge(xlT_made, 1)
                for t in range(cols.start // P, cols.stop // P):
                    pe.wait_ge(xl_made, b * T + t + 1)
                    last = nc.tensor.transpose(xt[:, t * P:(t + 1) * P], xl[:, b, t], ident)
                last.then_inc(xlT_psum, 1)

            def queries(i):
                b, cols, _, qw = QUERY_STEPS[i]
                pe.wait_ge(xlT_made, i + 1)
                if b:
                    pe.wait_ge(q_made, 1)
                nc.tensor.matmul(qw[:, cols], par("wqT"), xlT[:, b, cols], start=True, stop=True).then_inc(q_psum, 1)

            def scores(n):
                b, t = n // T, n % T
                if t == 0:
                    pe.wait_ge(kbd_made, b + 1)
                if n in (0, T // 2, T):
                    pe.wait_ge(q_made, 1 + n // (T // 2))
                if b:
                    pe.wait_ge(sd_made, n - T + 1)
                nc.tensor.matmul(SC[t][:], qT[:, b, t * P:(t + 1) * P], KBD[:, b].rearrange("p h k -> p (h k)"),
                                 start=True, stop=True).then_inc(scores_psum, 1)

            def transpose_probs(n):
                pe.wait_ge(pr_made, n + 1)
                if n >= 2:
                    pe.wait_ge(on_made, n - 1)
                elif n == 0:
                    pe.wait_ge(kbd_made, B)
                else:
                    pe.wait_ge(vbd_made, 2)
                for g in range(G):
                    last = nc.tensor.transpose(PT[n % 2][:, g * P:(g + 1) * P],
                                               pr[:, n // T, n % T, g * P:(g + 1) * P], ident)
                last.then_inc(pT_psum, 1)

            def values(n):
                pe.wait_ge(pT_made, n + 1)
                if n == 0:
                    pe.wait_ge(vbd_made, 2)
                for g in range(G):
                    last = nc.tensor.matmul(PT[n % 2][:, g * HG * VW:(g + 1) * HG * VW],
                                            pT[:, n // T, n % T, g * P:(g + 1) * P],
                                            VBD[:, n // T, g].rearrange("p j d -> p (j d)"), start=True, stop=True)
                last.then_inc(pv_psum, 1)

            def transpose_output(b):
                if b == 0:
                    pe.wait_ge(xlT_made, 3)
                else:
                    pe.wait_ge(oT_made, 1)
                for t in range(T):
                    pe.wait_ge(on_made, b * T + t + 1)
                    last = nc.tensor.transpose(XT[:, t * P:(t + 1) * P], on[:, b, t], ident)
                last.then_inc(oT_psum, 1)

            def combine(b):
                pe.wait_ge(oT_made, b + 1)
                if b == 0:
                    pe.wait_ge(q_made, 3)
                else:
                    pe.wait_ge(x1_made, 1)
                for t in range(T):
                    last = nc.tensor.matmul(QW[:, t * P:(t + 1) * P], oT[:, b, t * P:(t + 1) * P], par("woT"),
                                            start=True, stop=True)
                last.then_inc(wo_psum, 1)

            def transpose_xn(b):
                if b == 0:
                    pe.wait_ge(sd_made, T + 1)
                else:
                    pe.wait_ge(on_made, B * T)
                for t in range(T):
                    pe.wait_ge(xn_made, b * T + t + 1)
                    last = nc.tensor.transpose(XNT[b][:, t * P:(t + 1) * P], xn[:, b, t], ident)
                last.then_inc(xnT_psum, 1)

            def transpose_base(b):
                pe.wait_ge(base_made, T * (b + 1))
                if b == 0:
                    pe.wait_ge(on_made, B * T - 1)
                else:
                    pe.wait_ge(gates_in[1][0], 16)
                for t in range(T):
                    last = nc.tensor.transpose(BST[:, t * P:(t + 1) * P], base[:, b, t], ident)
                last.then_inc(baseT_psum, 1)

            def logits(b):
                pe.wait_ge(xh_made, b + 1)
                pe.wait_ge(xlo_made, b + 1)
                pe.wait_ge(wgl_made, 1)
                if b == 0:
                    pe.wait_ge(sd_made, T + 2)
                for t in range(T):
                    at, c = 2 * t * E, slice(t * P, (t + 1) * P)
                    nc.tensor.matmul(LGP[b][:, at:at + 2 * E], xh[:, b, c], wgs[:], start=True, stop=False,
                                     skip_group_check=True)
                    last = nc.tensor.matmul(LGP[b][:, at:at + E], xlo[:, b, c], wgs[:, 0:E], start=False, stop=True,
                                            skip_group_check=True)
                last.then_inc(lg_psum, 1)

            def transpose_gates(b):
                pe.wait_ge(gate_made, b + 1)
                if b:
                    pe.wait_ge(pg_made, 2)
                for t in range(T):
                    last = nc.tensor.transpose(GTP[b][0:E, t * P:(t + 1) * P], gate[:, b, t], ident)
                last.then_inc(gT_psum, 1)

            def spread_gates(i):
                b, e = divmod(i, 2)
                pe.wait_ge(gate_made, b + 1)
                if i == 0:
                    pe.wait_ge(baseT_made, 1)
                elif i == 1:
                    pe.wait_ge(x1_made, 2)
                elif i == 2:
                    pe.wait_ge(pg_made, 1)
                else:
                    pe.wait_ge(lg_made, 2)
                for t in range(T):
                    last = nc.tensor.transpose(GB[i][:, t * P:(t + 1) * P],
                                               gate[:, b, t, e:e + 1].to_broadcast([P, P]), ident)
                last.then_inc(gb_psum, 1)

            def bias_term(b):
                pe.wait_ge(gT_made, b + 1)
                pe.wait_ge(b2_in, 16)
                pe.wait_ge(x1_made, 2)
                nc.tensor.matmul(ACC[b][:], b2_sb[:], gT[:, b], start=True, stop=False, skip_group_check=True)

            def half_up(n, j, cols, dst, done, read):
                s, b = j % Q, j // Q
                if not isinstance(n, int) or n >= 2:
                    pe.wait_ge(read, n - 1)
                nc.tensor.matmul(dst[:], w1h[s][:, cols], xh[:, b], start=True, stop=False)
                nc.tensor.matmul(dst[:], w1h[s][:, cols], xlo[:, b], start=False, stop=False)
                nc.tensor.matmul(dst[:], w1l[s][:, cols], xh[:, b], start=False, stop=True).then_inc(done, 1)

            def odd_half(n, j):
                if isinstance(n, int) and n < Q:
                    pe.wait_ge(first_w1l, n + 1)
                if isinstance(n, int) and n == 0:
                    pe.wait_ge(xlo_made, 1)
                if isinstance(n, int) and n == 1:
                    pe.wait_ge(lg_made, 1)
                if isinstance(n, int) and n == Q:
                    pe.wait_ge(xlo_made, 2)
                half_up(n, j, slice(I, 2 * I), HB[j % 2], hb_psum, bt_made)

            def even_half(n, j):
                if isinstance(n, int) and n < 2:
                    pe.wait_ge(sd_made, B * T - 1 + n)
                half_up(n, j, slice(0, I), HA[j % 2], ha_psum, ge_made)

            def up(n, j):
                odd_half(n, j)
                even_half(n, j)

            def down(n, j, q, last=False):
                s, b = j % Q, j // Q
                pe.wait_ge(sg_made, n + 1)
                if b == 0:
                    pe.wait_ge(w2_in[s], q * 16 + 16)
                nc.tensor.matmul(ACC[b][:], w2s[s][:], sg[j % NS][:], start=False, stop=last,
                                 skip_group_check=True).then_inc(down_done, 1)

            pe.wait_ge(warm_set, 1)
            warm_up(WARM[0])
            pe.wait_ge(ctx_in, 16)
            nc.tensor.matmul(PT[0][:, 0:B * KV], cpar("wkT"), cpar("ctxT"), start=True,
                             stop=True).then_inc(kv_psum, 1)
            warm_up(WARM[1])
            pe.wait_ge(pk_in, 16)
            project(0)
            project(1)
            queries(0)
            pe.wait_ge(ctx4_made, 1)
            for b in range(B):
                last = nc.tensor.matmul(PT[1][:, b * D:(b + 1) * D], ctx4[:, b].rearrange("c g k -> c (g k)"),
                                        cpar("wvT"), start=True, stop=True)
            last.then_inc(kv_psum, 1)
            queries(1)
            scores(0)
            scores(1)
            scores(2)
            project(2)
            scores(3)
            queries(2)
            transpose_probs(0)
            transpose_probs(1)
            scores(4)
            values(0)
            values(1)
            scores(5)
            transpose_probs(2)
            transpose_probs(3)
            scores(6)
            values(2)
            values(3)
            scores(7)
            transpose_probs(4)
            transpose_probs(5)
            transpose_output(0)
            values(4)
            values(5)
            combine(0)
            transpose_probs(6)
            transpose_probs(7)
            values(6)
            values(7)
            transpose_output(1)
            pe.wait_ge(sd_made, B * T)
            warm_up(1)
            transpose_xn(0)
            combine(1)
            logits(0)
            pe.wait_ge(sd_made, B * T)
            warm_up(2)
            odd_half(0, 0)
            pe.wait_ge(sd_made, B * T)
            warm_up(1)
            even_half(0, 0)
            odd_half(1, 1)
            even_half(1, 1)
            transpose_base(0)
            odd_half(2, 2)
            transpose_gates(0)
            spread_gates(0)
            transpose_xn(1)
            spread_gates(1)
            even_half(2, 2)
            odd_half(3, 3)
            even_half(3, 3)
            logits(1)
            bias_term(0)
            down(0, 0, 0)
            up(4, 4)
            down(1, 1, 0)
            transpose_gates(1)
            spread_gates(2)
            spread_gates(3)
            bias_term(1)
            transpose_base(1)

            def step(q, k):
                n, j = q * (B * Q) + (Q + k), (Q + k) % (B * Q)
                down(n - 2, (j - 2) % (B * Q), q + (1 if k - 2 >= Q else 0))
                if Q <= k + 1 < B * Q:
                    pe.wait_ge(w1l_made, q * Q + (k + 1 - Q + 1))
                up(n + 1, (j + 1) % (B * Q))

            with pe.Fori(0, QUADS - 1) as q:
                for k in range(B * Q):
                    step(q, k)
            for k in range(Q - 1):
                step(QUADS - 1, k)
            for n in range(B * E - 3, B * E - 1):
                down(n, n % (B * Q), QUADS - 1, last=n == B * E - 2)
            for i, cols in enumerate(HALVES):
                pe.wait_ge(bt_made, B * E)
                pe.wait_ge(sg_made, B * E + i)
                nc.tensor.matmul(LAST[i][:, cols], w2s[Q - 1][:], sg[NS - 1][:, cols], start=True,
                                 stop=True).then_inc(down_done, 1)


def kernel(x, ctx_768, L0_xattn_Wq, L0_xattn_bq, L0_xattn_Wk, L0_xattn_bk, L0_xattn_Wv, L0_xattn_bv,
           L0_xattn_Wo, L0_xattn_bo, L0_ffn_norm_scale, L0_ffn_wg, L0_ffn_bg, L0_ffn_w1, L0_ffn_b1,
           L0_ffn_w2, L0_ffn_b2):
    import numpy as np
    import concourse.bacc as bacc
    from concourse.bass_utils import run_bass_kernel_spmd

    a = [np.asarray(v) for v in (x, ctx_768, L0_xattn_Wq, L0_xattn_bq, L0_xattn_Wk, L0_xattn_bk, L0_xattn_Wv,
                                 L0_xattn_bv, L0_xattn_Wo, L0_xattn_bo, L0_ffn_norm_scale, L0_ffn_wg, L0_ffn_bg,
                                 L0_ffn_w1, L0_ffn_b1, L0_ffn_w2, L0_ffn_b2)]
    x, ctx, wq, bq, wk, bk, wv, bv, wo, bo, ns, wg, bg, w1, b1, w2, b2 = a
    f = np.float32
    p = np.arange(P)
    ident = np.eye(P, dtype=f)
    head_mask = (p[:, None] // HD == np.arange(H)[None]).astype(f)
    group_mask = (p[:, None] // KV == np.arange(HG)[None]).astype(f)
    iota = np.broadcast_to(np.arange(E, dtype=f), (P, E))
    pack = np.concatenate([wq.T, wo.T, ident, wg, head_mask, group_mask, iota, bq[:, None], ns[:, None]], axis=1)
    ctx_pack = np.concatenate([
        np.concatenate([wk.T, bk[None]], axis=0),
        np.concatenate([wv.T, bv[None]], axis=0),
        np.concatenate([ctx.reshape(B * KV, C).T, np.ones((1, B * KV), f)], axis=0)], axis=1)
    w1s = w1.reshape(E, D, I, 2).transpose(1, 0, 3, 2).reshape(D, E * W1)
    b1s = b1.reshape(E, I, 2).transpose(1, 2, 0).reshape(I, 2 * E)
    rows = np.concatenate([bo, bg])
    arrays = {"x": x, "pack": pack, "ctx": ctx_pack, "rows": rows, "b2": b2, "w1": w1s, "w2": w2,
              "b1": b1s}
    arrays = {k: np.ascontiguousarray(v) for k, v in arrays.items()}
    nc = bacc.Bacc("TRN2", target_bir_lowering=False, num_devices=1)
    args = [nc.dram_tensor(f"in_{k}", v.shape, mybir.dt.from_np(v.dtype), kind="ExternalInput").ap()
            for k, v in arrays.items()]
    out = nc.dram_tensor("out", (D, B, N), FP32, kind="ExternalOutput").ap()
    build(nc, *args, out)
    r = run_bass_kernel_spmd(nc, [{f"in_{k}": v for k, v in arrays.items()}], core_ids=[0])
    got = r.results[0]["out"]
    return np.ascontiguousarray(got.reshape(D, B, T, P).transpose(1, 3, 2, 0).reshape(B, N, D))
```
